# Optimizing a Trainium2 kernel written in Bass

```python
import numpy as np
import jax
import jax.numpy as jnp

def _softmax(x, axis=-1):
    return jax.nn.softmax(x, axis=axis)

def _gelu(x):
    return jax.nn.gelu(x, approximate=True)

def _silu(x):
    return jax.nn.silu(x)

def _sigmoid(x):
    return jax.nn.sigmoid(x)

def _layernorm(x, axis=-1, eps=1e-05):
    m = jnp.mean(x, axis=axis, keepdims=True)
    v = jnp.var(x, axis=axis, keepdims=True)
    return (x - m) / jnp.sqrt(v + eps)

def _scatter_add(tgt, idx, src, axis=0):
    return tgt.at[idx].add(src)

def _segment_sum(src, seg, n):
    return jax.ops.segment_sum(src, seg, n)
kernel_name = 'mk_adj_resnorm_d1_adj_r2_172529'

def setup_inputs(seed: int=0):
    np.random.seed(seed)
    _w = jnp.asarray

    def _rec_inputs():
        import jax
        import jax.numpy as jnp
        _gk = jax.random.key(seed)
        x = 7.22e-05 + 1 * jax.random.normal(jax.random.fold_in(_gk, 1), (128, 128, 512), jnp.float32)
        _w = (1.0 + jnp.arange(128, dtype=jnp.float32)) ** (-0.5)
        _w = _w / _w.mean()
        _pij = jnp.clip(0.125 * _w[:, None] * _w[None, :], 0.0, 1.0)
        _a = jax.random.uniform(jax.random.fold_in(_gk, 2), (128, 128)) < _pij
        _a = jnp.logical_or(_a, jnp.eye(128, dtype=bool))
        _af = _a.astype(jnp.float32)
        adj = _af
        return (x, adj)
    x, adj = _rec_inputs()

    def _L0_gnn_setup():
        import jax, jax.numpy as jnp
        import numpy as np
        EPS = 1e-08

        def _row_stochastic_causal(A, causal_mask):
            A = A * causal_mask
            deg = jnp.maximum(A.sum(axis=-1, keepdims=True), EPS)
            return A / deg
        key = jax.random.key(seed)
        k = jax.random.split(key, 5)
        B, N, D = (4, 1024, 512)
        s = 1.0 / np.sqrt(D)
        h = jax.random.normal(k[0], (B, N, D), dtype=jnp.float32)
        W_lang = jax.random.normal(k[1], (D, D), dtype=jnp.float32) * s
        W_grav = jax.random.normal(k[2], (D, D), dtype=jnp.float32) * s
        W_V = jax.random.normal(k[3], (D, D), dtype=jnp.float32) * s
        W_O = jax.random.normal(k[4], (D, D), dtype=jnp.float32) * s
        causal_mask = jnp.tril(jnp.ones((N, N), dtype=jnp.float32))
        gate_logit = jnp.zeros((), jnp.float32)
        log_sigma = jnp.zeros((), jnp.float32)
        return {'h': h, 'causal_mask': causal_mask, 'W_lang': W_lang, 'W_grav': W_grav, 'W_V': W_V, 'W_O': W_O, 'gate_logit': gate_logit, 'log_sigma': log_sigma}
    _L0_gnn_all = _L0_gnn_setup()
    _L0_gnn_in = {k: v for k, v in _L0_gnn_all.items() if k in ('W_lang', 'W_grav', 'W_V', 'W_O', 'gate_logit', 'log_sigma')}
    del _L0_gnn_all
    return {'x': x, 'adj': adj, 'L0_gnn_W_lang': _L0_gnn_in['W_lang'], 'L0_gnn_W_grav': _L0_gnn_in['W_grav'], 'L0_gnn_W_V': _L0_gnn_in['W_V'], 'L0_gnn_W_O': _L0_gnn_in['W_O'], 'L0_gnn_gate_logit': _L0_gnn_in['gate_logit'], 'L0_gnn_log_sigma': _L0_gnn_in['log_sigma']}

def reference(x, adj, L0_gnn_W_lang, L0_gnn_W_grav, L0_gnn_W_V, L0_gnn_W_O, L0_gnn_gate_logit, L0_gnn_log_sigma):
    import jax
    import jax.numpy as jnp

    def _L0_gnn_ref(h, causal_mask, W_lang, W_grav, W_V, W_O, gate_logit, log_sigma):
        import jax, jax.numpy as jnp
        import numpy as np
        EPS = 1e-08

        def _row_stochastic_causal(A, causal_mask):
            A = A * causal_mask
            deg = jnp.maximum(A.sum(axis=-1, keepdims=True), EPS)
            return A / deg
        z_l = jnp.einsum('bnd,ed->bne', h, W_lang)
        z_g = jnp.einsum('bnd,ed->bne', h, W_grav)
        v = jnp.einsum('bnd,ed->bne', h, W_V)
        N = h.shape[-2]
        not_eye = 1.0 - jnp.eye(N, dtype=h.dtype)
        zn = z_l / jnp.maximum(jnp.linalg.norm(z_l, axis=-1, keepdims=True), EPS)
        A_l = jnp.maximum(jnp.einsum('bnd,bmd->bnm', zn, zn), 0.0) * not_eye
        sq = jnp.sum(z_g * z_g, axis=-1, keepdims=True)
        d2 = jnp.maximum(sq + jnp.swapaxes(sq, -1, -2) - 2.0 * jnp.einsum('bnd,bmd->bnm', z_g, z_g), 0.0)
        sigma = jnp.exp(log_sigma)
        A_g = jnp.exp(-d2 / (2.0 * sigma * sigma)) * not_eye
        K_l = _row_stochastic_causal(A_l, causal_mask)
        K_g = _row_stochastic_causal(A_g, causal_mask)
        w_l = jax.nn.sigmoid(gate_logit)
        K = w_l * K_l + (1.0 - w_l) * K_g
        out = jnp.einsum('bnm,bmd->bnd', K, v)
        return jnp.einsum('bnd,ed->bne', out, W_O)
    x = _layernorm(x + _L0_gnn_ref(x, adj, L0_gnn_W_lang, L0_gnn_W_grav, L0_gnn_W_V, L0_gnn_W_O, L0_gnn_gate_logit, L0_gnn_log_sigma), axis=-1)
    return x

_drawn_inputs = setup_inputs


def setup_inputs(seed=0):
    import zlib

    import numpy as np

    out = dict(_drawn_inputs(seed))
    spreads = {}
    factors = {}
    for name, (base, spread) in spreads.items():
        noise = np.random.default_rng([zlib.crc32(name.encode()), seed]).standard_normal(out[name].shape)
        drawn = base * np.exp(spread * noise) if base else spread * noise
        out[name] = jnp.asarray(drawn.astype(out[name].dtype))
    for name, factor in factors.items():
        out[name] = (out[name] * factor).astype(out[name].dtype)
    return out
```

```python
from contextlib import ExitStack

import concourse.bass as bass
from concourse import mybir

F32 = mybir.dt.float32
F32R = mybir.dt.float32r
I32 = mybir.dt.int32
ALU = mybir.AluOpType
ACT = mybir.ActivationFunctionType
AX_X = mybir.AxisListType.X

B, N, D = 128, 128, 512
P = 128
C = D // P
GB = 4
NG = B // GB
A = 2
RING = 4
EPS = 1e-8
LN_EPS = 1e-5
ROOT_MAGIC = float(0x5F3759DF)
NEWTON = 3

ROW_START = [sum(C - r for r in range(d)) for d in range(C)]
UBLOCKS = sum(C - d for d in range(C))

PROJECT_ORDER = [(e, a) for a in range(A) for e in (3, 0, 2, 1)]
NT = len(PROJECT_ORDER)
assert (GB + NT + GB) % RING == 0 and GB == RING


def attention_layernorm(nc, x, adj, w_lang, w_grav, w_v, w_o, gate_logit, log_sigma, y):
    with ExitStack() as ctx:
        def sb(name, shape, dt=F32):
            return ctx.enter_context(nc.sbuf_tensor(name, shape, dt))

        def psum(name, shape):
            return ctx.enter_context(nc.psum_tensor(name, shape, F32))

        def sem(name):
            return ctx.enter_context(nc.semaphore(name))

        u_hi = sb("u_hi", [P, A, UBLOCKS * P], F32R)
        u_lo = sb("u_lo", [P, A, UBLOCKS * P], F32R)
        wvo_hi = sb("wvo_hi", [P, C, D], F32R)
        wvo_lo = sb("wvo_lo", [P, C, D], F32R)
        x_nodes = [sb(f"x_nodes{i}", [P, GB, D]) for i in range(2)]
        xt_hi = [sb(f"xt_hi{i}", [P, C, GB, N], F32R) for i in range(2)]
        xt_lo = [sb(f"xt_lo{i}", [P, C, GB, N], F32R) for i in range(2)]
        t_hi = sb("t_hi", [P, C, GB, A, N], F32R)
        t_lo = sb("t_lo", [P, C, GB, A, N], F32R)
        v_hi = sb("v_hi", [P, GB, D], F32R)
        v_lo = sb("v_lo", [P, GB, D], F32R)
        y_nodes = sb("y_nodes", [P, GB, D])
        p_diag = sb("p_diag", [P, GB, A, N])
        p_l = sb("p_l", [P, GB, N])
        q_g = sb("q_g", [P, GB, N])
        s_l = sb("s_l", [P, GB, N])
        s_lr = sb("s_lr", [P, GB, N])
        d_g = sb("d_g", [P, GB, N])
        e_g = sb("e_g", [P, GB, N])
        edges = sb("edges", [P, A, GB, N])
        k_sum = sb("k_sum", [P, GB, N])
        kt_hi = sb("kt_hi", [P, GB, N], F32R)
        kt_lo = sb("kt_lo", [P, GB, N], F32R)
        diag = sb("diag", [P, GB, A])
        square = sb("square", [P, GB])
        square_half = sb("square_half", [P, GB])
        root = sb("root", [P, 3, GB])
        degree = sb("degree", [P, A, GB])
        coef = sb("coef", [P, 3, A, GB])
        row_scale = sb("row_scale", [P, A, GB])
        stats = sb("stats", [P, GB, 6])
        ln_part = sb("ln_part", [P, 5, GB])
        ln_mean = sb("ln_mean", [P, GB])
        ln_var = sb("ln_var", [P, GB])
        ln_var_half = sb("ln_var_half", [P, GB])
        ln_root = sb("ln_root", [P, 4, GB])
        ln_bias = sb("ln_bias", [P, GB])
        ident = sb("ident", [P, P])
        off_diag = sb("off_diag", [P, P])
        adj_sb = sb("adj_sb", [P, N])
        mask = sb("mask", [P, N])
        scalars = sb("scalars", [P, 8])
        three_halves = sb("three_halves", [P, GB])
        mix = sb("mix", [P, A, GB])
        w_raw = [sb(f"w_raw{i}", [P, C, D]) for i in range(2)]
        wo_t = sb("wo_t", [P, C, D])

        ring = [psum(f"ring{i}", [P, D]) for i in range(RING)]
        xt_ps = psum("xt_ps", [P, C, N])
        gram_ps = psum("gram_ps", [P, GB, A, N])
        turn_ps = psum("turn_ps", [P, GB, N])

        wl_loaded, wg_loaded, wv_loaded, wo_loaded = (sem(f"{n}_loaded") for n in ("wl", "wg", "wv", "wo"))
        adj_loaded, gate_loaded, sigma_loaded = sem("adj_loaded"), sem("gate_loaded"), sem("sigma_loaded")
        ident_zeroed, ident_made, off_made = sem("ident_zeroed"), sem("ident_made"), sem("off_made")
        ones_made, mask_made = sem("ones_made"), sem("mask_made")
        gate_exp, sigma_exp, scalar_step = sem("gate_exp"), sem("sigma_exp"), sem("scalar_step")
        wsum_done = sem("wsum_done")
        whi_done, wlo_done = sem("whi_done"), sem("wlo_done")
        wo_turned, wo_copied = sem("wo_turned"), sem("wo_copied")
        x_loaded = [[sem(f"x_loaded{i}_{b}") for b in range(GB)] for i in range(2)]
        y_stored = [sem(f"y_stored{b}") for b in range(GB)]
        xt_made, t_made, v_made, o_made = sem("xt_made"), sem("t_made"), sem("v_made"), sem("o_made")
        gram_made, turned = sem("gram_made"), sem("turned")
        xt_hi_made, xt_lo_made = sem("xt_hi_made"), sem("xt_lo_made")
        t_hi_made, t_lo_made = sem("t_hi_made"), sem("t_lo_made")
        v_hi_made, v_lo_made = sem("v_hi_made"), sem("v_lo_made")
        resid_made = sem("resid_made")
        pl_copied, diag_masked, diag_made, q_made = sem("pl_copied"), sem("diag_masked"), sem("diag_made"), sem("q_made")
        square_made, root_seed, root_step, root_made = sem("square_made"), sem("root_seed"), sem("root_step"), sem("root_made")
        s_made, sr_made, d_made, e_made = sem("s_made"), sem("sr_made"), sem("d_made"), sem("e_made")
        edges_made, degree_made = sem("edges_made"), sem("degree_made")
        coef_step, coef_made = sem("coef_step"), sem("coef_made")
        scaled_made, k_made, kt_hi_made, kt_lo_made = sem("scaled_made"), sem("k_made"), sem("kt_hi_made"), sem("kt_lo_made")
        stats_made, ln_part_made, var_made = sem("stats_made"), sem("ln_part_made"), sem("var_made")
        ln_seed, ln_step = sem("ln_seed"), sem("ln_step")
        ln_ready, normed = sem("ln_ready"), sem("normed")

        def by_rows(w):
            return w.rearrange("(c p) d -> p c d", p=P)

        def x_loads(g, parity):
            return 16 + (g - parity) * 8

        NS = NEWTON * 4

        block = ctx.enter_context(nc.Block())

        @block.sync
        def _(sp):
            sp.dma_start(w_raw[0][:], by_rows(w_lang)).then_inc(wl_loaded, 16)
            for b in range(GB):
                sp.dma_start(x_nodes[0][:, b], x[b]).then_inc(x_loaded[0][b], 16)
            sp.dma_start(w_raw[1][:], by_rows(w_grav)).then_inc(wg_loaded, 16)
            sp.dma_start(adj_sb[:], adj).then_inc(adj_loaded, 16)
            sp.dma_start(scalars[:, 0:1], gate_logit.partition_broadcast(P)).then_inc(gate_loaded, 16)
            sp.dma_start(scalars[:, 1:2], log_sigma.partition_broadcast(P)).then_inc(sigma_loaded, 16)
            sp.wait_ge(wsum_done, C)
            sp.dma_start(w_raw[0][:], by_rows(w_o)).then_inc(wo_loaded, 16)
            sp.wait_ge(wsum_done, 2 * C)
            sp.dma_start(w_raw[1][:], by_rows(w_v)).then_inc(wv_loaded, 16)
            for b in range(GB):
                sp.dma_start(x_nodes[1][:, b], x[GB + b]).then_inc(x_loaded[1][b], 16)

            x_pairs = x.rearrange("(i q b) n d -> i q b n d", q=2, b=GB)
            y_pairs = y.rearrange("(i q b) n d -> i q b n d", q=2, b=GB)

            def store(pair, parity):
                for b in range(GB):
                    sp.wait_ge(normed, GB * (2 * pair + parity) + b + 1)
                    sp.dma_start(y_pairs[pair, parity, b], y_nodes[:, b]).then_inc(y_stored[b], 16)

            with sp.Fori(0, NG // 2 - 1) as pair:
                for parity in range(2):
                    for b in range(GB):
                        sp.wait_ge(resid_made, GB * (2 * pair + parity) + b + 1)
                        sp.dma_start(x_nodes[parity][:, b], x_pairs[pair + 1, parity, b])\
                            .then_inc(x_loaded[parity][b], 16)
                    store(pair, parity)
            for parity in range(2):
                store(NG // 2 - 1, parity)
            for b in range(GB):
                sp.wait_ge(y_stored[b], 16 * NG)

        @block.tensor
        def _(pe):
            def product(out, pairs):
                for n, (lhsT, rhs) in enumerate(pairs):
                    last = nc.tensor.matmul(out, lhsT, rhs, start=(n == 0), stop=(n == len(pairs) - 1))
                return last

            def turn_x(g, parity, b):
                pe.wait_ge(x_loaded[parity][b], x_loads(g, parity))
                for c in range(C):
                    last = nc.tensor.transpose(xt_ps[:, c], x_nodes[parity][:, b, c * P:(c + 1) * P], ident[:])
                last.then_inc(xt_made, 1)

            def project(g, parity, t):
                e, a = PROJECT_ORDER[t]
                pairs = []
                for d in range(e + 1):
                    at = (ROW_START[d] + e - d) * P
                    hi, lo = u_hi[:, a, at:at + P], u_lo[:, a, at:at + P]
                    xh = xt_hi[parity][:, d].rearrange("p b n -> p (b n)")
                    xl = xt_lo[parity][:, d].rearrange("p b n -> p (b n)")
                    pairs += [(hi, xh), (hi, xl), (lo, xh)]
                product(ring[t % RING][:], pairs).then_inc(t_made, 1)

            def value(g, parity, b):
                pairs = []
                for c in range(C):
                    xh, xl = xt_hi[parity][:, c, b], xt_lo[parity][:, c, b]
                    pairs += [(xh, wvo_hi[:, c]), (xh, wvo_lo[:, c]), (xl, wvo_hi[:, c])]
                product(ring[b][:], pairs).then_inc(v_made, 1)

            def gram(g, parity, b):
                pairs = []
                for c in range(C):
                    xh, xl = xt_hi[parity][:, c, b], xt_lo[parity][:, c, b]
                    th = t_hi[:, c, b].rearrange("p a n -> p (a n)")
                    tl = t_lo[:, c, b].rearrange("p a n -> p (a n)")
                    pairs += [(xh, th), (xh, tl), (xl, th)]
                product(gram_ps[:, b].rearrange("p a n -> p (a n)"), pairs).then_inc(gram_made, 1)

            def aggregate(g, b):
                product(ring[b][:], [(kt_hi[:, b], v_hi[:, b]), (kt_hi[:, b], v_lo[:, b]),
                                     (kt_lo[:, b], v_hi[:, b])]).then_inc(o_made, 1)

            def turn(m):
                for b in range(GB):
                    last = nc.tensor.transpose(turn_ps[:, b], m[:, b], ident[:])
                last.then_inc(turned, 1)

            def first_x():
                for b in range(GB):
                    if b:
                        pe.wait_ge(xt_lo_made, b)
                    turn_x(0, 0, b)

            pe.wait_ge(ident_made, 1)
            for a, loaded in enumerate((wl_loaded, wg_loaded)):
                pe.wait_ge(loaded, 16)
                for d in range(C):
                    if a:
                        pe.wait_ge(wlo_done, d + 1)
                    product(ring[d][:, d * P:], [(w_raw[a][:, k, d * P:(d + 1) * P], w_raw[a][:, k, d * P:])
                                                 for k in range(C)]).then_inc(wsum_done, 1)
                if a == 0:
                    first_x()
            pe.wait_ge(wo_loaded, 16)
            for k in range(C):
                pe.wait_ge(wlo_done, C + k + 1)
                for e in range(C):
                    last = nc.tensor.transpose(ring[k][:, e * P:(e + 1) * P], w_raw[0][:, e, k * P:(k + 1) * P], ident[:])
                last.then_inc(wo_turned, 1)
            pe.wait_ge(wv_loaded, 16)
            pe.wait_ge(wo_copied, C)
            for d in range(C):
                product(ring[d][:], [(w_raw[1][:, k, d * P:(d + 1) * P], wo_t[:, k]) for k in range(C)])\
                    .then_inc(wsum_done, 1)

            def projects(g, parity, after_setup=False):
                pe.wait_ge(xt_hi_made, GB * (g + 1))
                pe.wait_ge(xt_lo_made, GB * (g + 1))
                for t in range(NT):
                    if t >= RING:
                        pe.wait_ge(t_lo_made, NT * g + t - RING + 1)
                    elif after_setup:
                        pe.wait_ge(wlo_done, 2 * C + t + 1)
                    else:
                        pe.wait_ge(v_lo_made, GB * (g - 1) + t + 1)
                    project(g, parity, t)
                    yield t

            for _ in projects(0, 0, after_setup=True):
                pass

            def iteration(g, parity, first=False, last=False):
                pe.wait_ge(t_hi_made, NT * (g + 1))
                pe.wait_ge(t_lo_made, NT * (g + 1))
                if not first:
                    pe.wait_ge(pl_copied, g)
                    pe.wait_ge(q_made, g)
                for b in range(GB):
                    gram(g, parity, b)
                for b in range(GB):
                    if not last:
                        pe.wait_ge(xt_lo_made, GB * (g + 1) + b)
                        turn_x(g + 1, 1 - parity, b)
                    if first:
                        pe.wait_ge(t_lo_made, NT * g + NT - RING + b + 1)
                    else:
                        pe.wait_ge(resid_made, GB * (g - 1) + b + 1)
                    value(g, parity, b)
                    if b == 0:
                        pe.wait_ge(pl_copied, g + 1)
                        if not first:
                            pe.wait_ge(kt_lo_made, g)
                        turn(p_l)
                    if b == 1:
                        pe.wait_ge(q_made, g + 1)
                        pe.wait_ge(s_made, g + 1)
                        turn(q_g)
                    if b == 2:
                        pe.wait_ge(sr_made, g + 1)
                        pe.wait_ge(d_made, g + 1)
                        turn(s_lr)

                def turn_k():
                    pe.wait_ge(k_made, g + 1)
                    pe.wait_ge(edges_made, 2 * g + 2)
                    turn(k_sum)

                if last:
                    turn_k()
                else:
                    for t in projects(g + 1, 1 - parity):
                        if t == 5:
                            turn_k()
                pe.wait_ge(kt_hi_made, g + 1)
                pe.wait_ge(kt_lo_made, g + 1)
                for b in range(GB):
                    if last:
                        pe.wait_ge(v_lo_made, GB * g + b + 1)
                    else:
                        pe.wait_ge(t_lo_made, NT * (g + 1) + NT - RING + b + 1)
                    aggregate(g, b)

            iteration(0, 0, first=True)
            with pe.Fori(1, NG - 1, 2) as i:
                iteration(i, 1)
                iteration(i + 1, 0)
            iteration(NG - 1, 1, last=True)

        @block.scalar
        def _(act):
            def hi_of(out, in_):
                return nc.scalar.activation(out, in_, ACT.Copy)

            def split_x(g, parity, b):
                act.wait_ge(xt_made, GB * g + b + 1)
                hi_of(xt_hi[parity][:, :, b], xt_ps[:]).then_inc(xt_hi_made, 1)

            def split_t(g, t):
                e, a = PROJECT_ORDER[t]
                act.wait_ge(t_made, NT * g + t + 1)
                hi_of(t_hi[:, e, :, a], ring[t % RING][:].rearrange("p (b n) -> p b n", b=GB)).then_inc(t_hi_made, 1)

            def split_v(g, b):
                act.wait_ge(v_made, GB * g + b + 1)
                hi_of(v_hi[:, b], ring[b][:]).then_inc(v_hi_made, 1)

            act.wait_ge(gate_loaded, 16)
            nc.scalar.activation(scalars[:, 2:3], scalars[:, 0:1], ACT.Exp, scale=-1.0).then_inc(gate_exp, 1)
            act.wait_ge(sigma_loaded, 16)
            nc.scalar.activation(scalars[:, 3:4], scalars[:, 1:2], ACT.Exp).then_inc(sigma_exp, 1)
            for a in range(A):
                for d in range(C):
                    act.wait_ge(wsum_done, C * a + d + 1)
                    at = ROW_START[d] * P
                    own, rest = (d * P, (d + 1) * P), ((d + 1) * P, D)
                    n = (C - 1 - d) * P
                    if n:
                        hi_of(u_hi[:, a, at + P:at + P + n], ring[d][:, rest[0]:rest[1]]).then_inc(whi_done, 1)
                    nc.scalar.activation(u_hi[:, a, at:at + P], ring[d][:, own[0]:own[1]], ACT.Copy, scale=0.5)\
                        .then_inc(whi_done, 1)
                if a == 0:
                    for b in range(GB):
                        split_x(0, 0, b)
            for k in range(C):
                act.wait_ge(wo_turned, k + 1)
                nc.scalar.activation(wo_t[:, k], ring[k][:], ACT.Copy).then_inc(wo_copied, 1)
            for d in range(C):
                act.wait_ge(wsum_done, 2 * C + d + 1)
                hi_of(wvo_hi[:, d], ring[d][:]).then_inc(whi_done, 1)
            for t in range(NT):
                split_t(0, t)

            def copy_pl(g):
                act.wait_ge(gram_made, GB * (g + 1))
                act.wait_ge(diag_masked, 2 * (g + 1))
                nc.scalar.activation(p_l[:], gram_ps[:, :, 0], ACT.Copy).then_inc(pl_copied, 1)

            def exp_g(g):
                act.wait_ge(d_made, g + 1)
                nc.scalar.activation(e_g[:], d_g[:], ACT.Exp, scale=scalars[:, 6:7]).then_inc(e_made, 1)

            def split_k(g):
                act.wait_ge(turned, 4 * (g + 1))
                hi_of(kt_hi[:], turn_ps[:]).then_inc(kt_hi_made, 1)

            def normalise(g, b):
                act.wait_ge(ln_ready, g + 1)
                nc.scalar.activation(y_nodes[:, b], y_nodes[:, b], ACT.Identity, scale=ln_root[:, 3, b:b + 1],
                                     bias=ln_bias[:, b:b + 1]).then_inc(normed, 1)

            def iteration(g, parity, first=False, last=False):
                copy_pl(g)
                for b in range(GB):
                    if not last:
                        split_x(g + 1, 1 - parity, b)
                    split_v(g, b)
                    if not first:
                        normalise(g - 1, b)
                    if b == 1:
                        exp_g(g)
                if last:
                    split_k(g)
                else:
                    for t in range(NT):
                        split_t(g + 1, t)
                        if t == 5:
                            split_k(g)

            act.wait_ge(scalar_step, 4)
            iteration(0, 0, first=True)
            with act.Fori(1, NG - 1, 2) as i:
                iteration(i, 1)
                iteration(i + 1, 0)
            iteration(NG - 1, 1, last=True)
            for b in range(GB):
                normalise(NG - 1, b)

        @block.vector
        def _(dve):
            def lo_of(out, whole, hi):
                return nc.vector.tensor_tensor(out, whole, hi.bitcast(F32), ALU.subtract)

            def split_x(g, parity, b):
                dve.wait_ge(xt_hi_made, GB * g + b + 1)
                lo_of(xt_lo[parity][:, :, b], xt_ps[:], xt_hi[parity][:, :, b]).then_inc(xt_lo_made, 1)

            def split_t(g, t):
                e, a = PROJECT_ORDER[t]
                dve.wait_ge(t_hi_made, NT * g + t + 1)
                lo_of(t_lo[:, e, :, a], ring[t % RING][:].rearrange("p (b n) -> p b n", b=GB), t_hi[:, e, :, a])\
                    .then_inc(t_lo_made, 1)

            def split_v(g, b):
                dve.wait_ge(v_hi_made, GB * g + b + 1)
                lo_of(v_lo[:, b], ring[b][:], v_hi[:, b]).then_inc(v_lo_made, 1)

            def over_nodes(v):
                return v.unsqueeze(2).broadcast_to([P, GB, N])

            nc.vector.memset(row_scale[:, 1], 1.0).then_inc(ones_made, 1)
            nc.vector.memset(three_halves[:], 1.5).then_inc(ones_made, 1)
            dve.wait_ge(gate_exp, 1)
            dve.wait_ge(sigma_exp, 1)
            nc.vector.tensor_scalar(scalars[:, 4:5], scalars[:, 2:3], 1.0, None, ALU.add).then_inc(scalar_step, 1)
            nc.vector.tensor_tensor(scalars[:, 5:6], scalars[:, 3:4], scalars[:, 3:4], ALU.mult).then_inc(scalar_step, 1)
            dve.wait_ge(scalar_step, 2)
            nc.vector.reciprocal(scalars[:, 7:8], scalars[:, 4:5]).then_inc(scalar_step, 1)
            nc.vector.reciprocal(scalars[:, 6:7], scalars[:, 5:6]).then_inc(scalar_step, 1)
            dve.wait_ge(scalar_step, 4)
            dve.wait_ge(ones_made, 2)
            nc.vector.tensor_scalar(mix[:, 0], row_scale[:, 1], scalars[:, 7:8], None, ALU.mult).then_inc(scalar_step, 1)
            dve.wait_ge(scalar_step, 5)
            nc.vector.tensor_scalar(mix[:, 1], mix[:, 0], -1.0, 1.0, ALU.mult, ALU.add).then_inc(scalar_step, 1)
            dve.wait_ge(adj_loaded, 16)
            dve.wait_ge(ident_made, 1)
            nc.vector.tensor_scalar(off_diag[:], ident[:], -1.0, 1.0, ALU.mult, ALU.add).then_inc(off_made, 1)
            dve.wait_ge(off_made, 1)
            nc.vector.tensor_tensor(mask[:], adj_sb[:], off_diag[:], ALU.mult).then_inc(mask_made, 1)

            hi_parts = 0
            for a in range(A):
                for d in range(C):
                    at = ROW_START[d] * P
                    n = (C - 1 - d) * P
                    hi_parts += 2 if n else 1
                    dve.wait_ge(whi_done, hi_parts)
                    if n:
                        lo_of(u_lo[:, a, at + P:at + P + n], ring[d][:, (d + 1) * P:], u_hi[:, a, at + P:at + P + n])
                    nc.vector.scalar_tensor_tensor(out=u_lo[:, a, at:at + P], in0=ring[d][:, d * P:(d + 1) * P],
                                                   scalar=0.5, in1=u_hi[:, a, at:at + P].bitcast(F32),
                                                   op0=ALU.mult, op1=ALU.subtract).then_inc(wlo_done, 1)
                if a == 0:
                    for b in range(GB):
                        split_x(0, 0, b)
            for d in range(C):
                dve.wait_ge(whi_done, hi_parts + d + 1)
                lo_of(wvo_lo[:, d], ring[d][:], wvo_hi[:, d]).then_inc(wlo_done, 1)
            for t in range(NT):
                split_t(0, t)

            def mask_diagonal(g):
                for half in range(2):
                    graphs = slice(2 * half, 2 * half + 2)
                    dve.wait_ge(gram_made, GB * g + 2 * half + 2)
                    nc.vector.tensor_tensor(p_diag[:, graphs].rearrange("p b a n -> p (b a) n"),
                                            gram_ps[:, graphs].rearrange("p b a n -> p (b a) n"),
                                            ident[:].unsqueeze(1).broadcast_to([P, 2 * A, N]), ALU.mult)\
                        .then_inc(diag_masked, 1)

            def diagonal(g):
                dve.wait_ge(diag_masked, 2 * (g + 1))
                nc.vector.tensor_reduce(diag[:], p_diag[:], AX_X, ALU.add).then_inc(diag_made, 1)
                dve.wait_ge(diag_made, g + 1)
                nc.vector.tensor_scalar(square[:], diag[:, :, 0], 2.0, EPS * EPS, ALU.mult, ALU.max)\
                    .then_inc(square_made, 1)
                dve.wait_ge(square_made, g + 1)
                nc.vector.tensor_scalar(square_half[:], square[:], -0.5, None, ALU.mult)
                nc.vector.tensor_scalar(root[:, 0].bitcast(I32), square[:].bitcast(I32), -0.5, ROOT_MAGIC,
                                        ALU.mult, ALU.add).then_inc(root_seed, 1)

            def make_q(g):
                dve.wait_ge(pl_copied, g + 1)
                nc.vector.tensor_tensor(q_g[:], gram_ps[:, :, 1], over_nodes(diag[:, :, 1]), ALU.subtract)\
                    .then_inc(q_made, 1)

            def add_s(g):
                dve.wait_ge(turned, 4 * g + 1)
                nc.vector.tensor_tensor(s_l[:], turn_ps[:], p_l[:], ALU.add).then_inc(s_made, 1)

            def add_d(g):
                dve.wait_ge(turned, 4 * g + 2)
                nc.vector.tensor_tensor(d_g[:], turn_ps[:], q_g[:], ALU.add).then_inc(d_made, 1)

            def edges_g(g):
                dve.wait_ge(e_made, g + 1)
                nc.vector.scalar_tensor_tensor(out=edges[:, 1], in0=e_g[:], scalar=1.0,
                                               in1=mask[:].unsqueeze(1).broadcast_to([P, GB, N]),
                                               op0=ALU.min, op1=ALU.mult).then_inc(edges_made, 1)

            def edges_l(g):
                dve.wait_ge(turned, 4 * g + 3)
                nc.vector.scalar_tensor_tensor(out=edges[:, 0], in0=turn_ps[:], scalar=0.0,
                                               in1=mask[:].unsqueeze(1).broadcast_to([P, GB, N]),
                                               op0=ALU.max, op1=ALU.mult).then_inc(edges_made, 1)

            def coefficients(g):
                step = 4 * g
                dve.wait_ge(edges_made, 2 * g + 2)
                nc.vector.tensor_reduce(degree[:], edges[:], AX_X, ALU.add).then_inc(degree_made, 1)
                dve.wait_ge(degree_made, g + 1)
                nc.vector.tensor_tensor(coef[:, 0], degree[:], row_scale[:], ALU.mult).then_inc(coef_step, 1)
                dve.wait_ge(coef_step, step + 1)
                nc.vector.tensor_scalar(coef[:, 1], coef[:, 0], EPS, None, ALU.max).then_inc(coef_step, 1)
                dve.wait_ge(coef_step, step + 2)
                nc.vector.reciprocal(coef[:, 0], coef[:, 1]).then_inc(coef_step, 1)
                dve.wait_ge(coef_step, step + 3)
                nc.vector.tensor_tensor(coef[:, 1], coef[:, 0], row_scale[:], ALU.mult).then_inc(coef_step, 1)
                dve.wait_ge(coef_step, step + 4)
                nc.vector.tensor_tensor(coef[:, 2], coef[:, 1], mix[:], ALU.mult).then_inc(coef_made, 1)

            def sum_k(g):
                dve.wait_ge(scaled_made, g + 1)
                nc.vector.tensor_tensor(k_sum[:], edges[:, 0], edges[:, 1], ALU.add).then_inc(k_made, 1)

            def split_k(g):
                dve.wait_ge(kt_hi_made, g + 1)
                lo_of(kt_lo[:], turn_ps[:], kt_hi[:]).then_inc(kt_lo_made, 1)

            def residual(g, parity, first):
                for b in range(GB):
                    dve.wait_ge(o_made, GB * g + b + 1)
                    if not first:
                        dve.wait_ge(y_stored[b], 16 * g)
                    nc.vector.tensor_tensor(y_nodes[:, b], ring[b][:], x_nodes[parity][:, b], ALU.add)\
                        .then_inc(resid_made, 1)
                    if b:
                        dve.wait_ge(resid_made, GB * g + b)
                        nc.vector.bn_stats(stats[:, b - 1], y_nodes[:, b - 1]).then_inc(stats_made, 1)
                dve.wait_ge(resid_made, GB * (g + 1))
                nc.vector.bn_stats(stats[:, GB - 1], y_nodes[:, GB - 1]).then_inc(stats_made, 1)
                dve.wait_ge(stats_made, GB * (g + 1))
                step = 5 * g
                nc.vector.tensor_tensor(ln_part[:, 0], stats[:, :, 1], stats[:, :, 4], ALU.add).then_inc(ln_part_made, 1)
                nc.vector.tensor_tensor(ln_part[:, 1], stats[:, :, 1], stats[:, :, 4], ALU.subtract)\
                    .then_inc(ln_part_made, 1)
                nc.vector.tensor_tensor(ln_part[:, 2], stats[:, :, 2], stats[:, :, 5], ALU.add).then_inc(ln_part_made, 1)
                dve.wait_ge(ln_part_made, step + 3)
                nc.vector.tensor_tensor(ln_part[:, 3], ln_part[:, 1], ln_part[:, 1], ALU.mult).then_inc(ln_part_made, 1)
                nc.vector.tensor_scalar(ln_part[:, 4], ln_part[:, 2], 1.0 / D, LN_EPS, ALU.mult, ALU.add)\
                    .then_inc(ln_part_made, 1)
                nc.vector.tensor_scalar(ln_mean[:], ln_part[:, 0], -0.5, None, ALU.mult)
                dve.wait_ge(ln_part_made, step + 5)
                nc.vector.scalar_tensor_tensor(out=ln_var[:], in0=ln_part[:, 3], scalar=0.25, in1=ln_part[:, 4],
                                               op0=ALU.mult, op1=ALU.add).then_inc(var_made, 1)
                dve.wait_ge(var_made, g + 1)
                nc.vector.tensor_scalar(ln_var_half[:], ln_var[:], -0.5, None, ALU.mult)
                nc.vector.tensor_scalar(ln_root[:, 0].bitcast(I32), ln_var[:].bitcast(I32), -0.5, ROOT_MAGIC,
                                        ALU.mult, ALU.add).then_inc(ln_seed, 1)

            def iteration(g, parity, first=False, last=False):
                mask_diagonal(g)
                for b in range(GB):
                    if not last:
                        split_x(g + 1, 1 - parity, b)
                    if b == 0:
                        diagonal(g)
                        make_q(g)
                    split_v(g, b)
                    if b == 0:
                        add_s(g)
                    if b == 1:
                        add_d(g)
                    if b == 2:
                        edges_g(g)
                        edges_l(g)
                coefficients(g)
                if last:
                    sum_k(g)
                    split_k(g)
                else:
                    for t in range(NT):
                        split_t(g + 1, t)
                        if t == 3:
                            sum_k(g)
                        if t == 5:
                            split_k(g)
                residual(g, parity, first)

            dve.wait_ge(scalar_step, 6)
            dve.wait_ge(mask_made, 1)
            iteration(0, 0, first=True)
            with dve.Fori(1, NG - 1, 2) as i:
                iteration(i, 1)
                iteration(i + 1, 0)
            iteration(NG - 1, 1, last=True)

        @block.gpsimd
        def _(pool):
            nc.gpsimd.memset(ident[:], 0.0).then_inc(ident_zeroed, 1)
            pool.wait_ge(ident_zeroed, 1)
            nc.gpsimd.affine_select(out=ident[:], in_=ident[:], compare_op=ALU.not_equal, fill=1.0, base=0,
                                    pattern=[[-1, P]], channel_multiplier=1).then_inc(ident_made, 1)

            def inverse_root(value_half, guess, out, step, base):
                for n in range(NEWTON):
                    at = base + 4 * n
                    if n:
                        pool.wait_ge(step, at)
                    nc.gpsimd.tensor_tensor(guess[:, 1], guess[:, 0], guess[:, 0], ALU.mult).then_inc(step, 1)
                    pool.wait_ge(step, at + 1)
                    nc.gpsimd.tensor_tensor(guess[:, 2], guess[:, 1], value_half, ALU.mult).then_inc(step, 1)
                    pool.wait_ge(step, at + 2)
                    nc.gpsimd.tensor_tensor(guess[:, 1], guess[:, 2], three_halves[:], ALU.add).then_inc(step, 1)
                    pool.wait_ge(step, at + 3)
                    nc.gpsimd.tensor_tensor(out if n == NEWTON - 1 else guess[:, 0], guess[:, 0], guess[:, 1],
                                            ALU.mult).then_inc(step, 1)
                pool.wait_ge(step, base + NS)

            def layernorm_factors(g):
                pool.wait_ge(ln_seed, g + 1)
                inverse_root(ln_var_half[:], ln_root, ln_root[:, 3], ln_step, NS * g)
                nc.gpsimd.tensor_tensor(ln_bias[:], ln_mean[:], ln_root[:, 3], ALU.mult).then_inc(ln_ready, 1)

            def node_scale(g):
                pool.wait_ge(root_seed, g + 1)
                inverse_root(square_half[:], root, row_scale[:, 0], root_step, NS * g)

            def scale_s(g):
                pool.wait_ge(s_made, g + 1)
                nc.gpsimd.tensor_tensor(s_lr[:], s_l[:], row_scale[:, 0].unsqueeze(2).broadcast_to([P, GB, N]),
                                        ALU.mult).then_inc(sr_made, 1)

            def scale_edges(g):
                pool.wait_ge(coef_made, g + 1)
                nc.gpsimd.tensor_tensor(edges[:], edges[:], coef[:, 2].unsqueeze(3).broadcast_to([P, A, GB, N]),
                                        ALU.mult).then_inc(scaled_made, 1)

            pool.wait_ge(ones_made, 2)

            def iteration(g, first=False):
                if not first:
                    layernorm_factors(g - 1)
                node_scale(g)
                scale_s(g)
                scale_edges(g)

            iteration(0, first=True)
            with pool.Fori(1, NG - 1, 2) as i:
                iteration(i)
                iteration(i + 1)
            iteration(NG - 1)
            layernorm_factors(NG - 1)


_INS = ["x", "adj", "L0_gnn_W_lang", "L0_gnn_W_grav", "L0_gnn_W_V", "L0_gnn_W_O", "L0_gnn_gate_logit",
        "L0_gnn_log_sigma"]


def kernel(**inputs):
    import numpy as _np
    import concourse.bacc as _bacc
    from concourse.bass_utils import run_bass_kernel_spmd as _run

    nc = _bacc.Bacc("TRN2", target_bir_lowering=False, num_devices=1)
    arrays, args = {}, []
    for name in _INS:
        a = _np.ascontiguousarray(inputs[name])
        if a.ndim == 0:
            a = a.reshape(1)
        arrays[f"in_{name}"] = a
        args.append(nc.dram_tensor(f"in_{name}", a.shape, mybir.dt.from_np(a.dtype), kind="ExternalInput").ap())
    y = nc.dram_tensor("out_y", (B, N, D), F32, kind="ExternalOutput").ap()
    attention_layernorm(nc, *args, y)
    r = _run(nc, [arrays], core_ids=[0])
    return r.results[0]["out_y"]
```

```python
from contextlib import ExitStack

import concourse.bass as bass
from concourse import mybir

F32 = mybir.dt.float32
F32R = mybir.dt.float32r
I32 = mybir.dt.int32
ALU = mybir.AluOpType
ACT = mybir.ActivationFunctionType
AX_X = mybir.AxisListType.X

B, N, D = 128, 128, 512
P = 128
C = D // P
GB = 4
NG = B // GB
A = 2
RING = 4
EPS = 1e-8
LN_EPS = 1e-5
ROOT_MAGIC = float(0x5F3759DF)
NEWTON = 3

ROW_START = [sum(C - r for r in range(d)) for d in range(C)]
UBLOCKS = sum(C - d for d in range(C))
G_FROM = [min(d * P, D - 256) for d in range(C)]

PROJECT_ORDER = [(e, a) for a in range(A) for e in (3, 0, 2, 1)]
NT = len(PROJECT_ORDER)
assert (GB + NT + GB) % RING == 0 and GB == RING


def attention_layernorm(nc, x, adj, w_lang, w_grav, w_v, w_o, gate_logit, log_sigma, y):
    with ExitStack() as ctx:
        def sb(name, shape, dt=F32):
            return ctx.enter_context(nc.sbuf_tensor(name, shape, dt))

        def psum(name, shape):
            return ctx.enter_context(nc.psum_tensor(name, shape, F32))

        def sem(name):
            return ctx.enter_context(nc.semaphore(name))

        u_hi = sb("u_hi", [P, A, UBLOCKS * P], F32R)
        u_lo = sb("u_lo", [P, A, UBLOCKS * P], F32R)
        wvo_hi = sb("wvo_hi", [P, C, D], F32R)
        wvo_lo = sb("wvo_lo", [P, C, D], F32R)
        x_nodes = [sb(f"x_nodes{i}", [P, GB, D]) for i in range(2)]
        xt_hi = [sb(f"xt_hi{i}", [P, C, GB, N], F32R) for i in range(2)]
        xt_lo = [sb(f"xt_lo{i}", [P, C, GB, N], F32R) for i in range(2)]
        t_hi = sb("t_hi", [P, C, GB, A, N], F32R)
        t_lo = sb("t_lo", [P, C, GB, A, N], F32R)
        v_hi = sb("v_hi", [P, GB, D], F32R)
        v_lo = sb("v_lo", [P, GB, D], F32R)
        y_nodes = sb("y_nodes", [P, GB, D])
        p_diag = sb("p_diag", [P, GB, A, N])
        p_l = sb("p_l", [P, GB, N])
        q_g = sb("q_g", [P, GB, N])
        s_l = sb("s_l", [P, GB, N])
        m_l = sb("m_l", [P, GB, N])
        scale_rows = sb("scale_rows", [P, GB, N])
        scale_dram = nc.dram_tensor("scale_dram", (GB, N), F32).ap()
        d_g = sb("d_g", [P, GB, N])
        e_g = sb("e_g", [P, GB, N])
        edges = sb("edges", [P, A, GB, N])
        k_sum = sb("k_sum", [P, GB, N])
        kt_hi = sb("kt_hi", [P, GB, N], F32R)
        kt_lo = sb("kt_lo", [P, GB, N], F32R)
        diag = sb("diag", [P, GB, A])
        square = sb("square", [P, GB])
        square_half = sb("square_half", [P, GB])
        root = sb("root", [P, 3, GB])
        degree = sb("degree", [P, A, GB])
        coef = sb("coef", [P, 3, A, GB])
        row_scale = sb("row_scale", [P, A, GB])
        stats = sb("stats", [P, GB, 6])
        ln_part = sb("ln_part", [P, 5, GB])
        ln_mean = sb("ln_mean", [P, GB])
        ln_var = sb("ln_var", [P, GB])
        ln_var_half = sb("ln_var_half", [P, GB])
        ln_root = sb("ln_root", [P, 4, GB])
        ln_bias = sb("ln_bias", [P, GB])
        ident = sb("ident", [P, P])
        off_diag = sb("off_diag", [P, P])
        adj_sb = sb("adj_sb", [P, N])
        mask = sb("mask", [P, N])
        scalars = sb("scalars", [P, 8])
        three_halves = sb("three_halves", [P, GB])
        mix = sb("mix", [P, A, GB])
        wl_raw, wg_raw, wv_raw, wo_raw = (sb(f"{n}_raw", [P, C, D]) for n in ("wl", "wg", "wv", "wo"))
        def halves(t):
            flat = t[:].rearrange("p c b a n -> p (c b a n)")
            return tuple(flat[:, i * C * D:(i + 1) * C * D].rearrange("p (c d) -> p c d", c=C) for i in range(2))
        wl_hi, wl_lo = halves(t_hi)
        wg_hi, wg_lo = halves(t_lo)
        wot_hi, wot_lo = (t[1][:].rearrange("p c b n -> p c (b n)") for t in (xt_hi, xt_lo))
        wv_hi, wv_lo = v_hi, v_lo

        ring = [psum(f"ring{i}", [P, D]) for i in range(RING)]
        xt_ps = psum("xt_ps", [P, C, N])
        gram_ps = psum("gram_ps", [P, GB, A, N])
        turn_ps = psum("turn_ps", [P, GB, N])
        gram_flat = gram_ps[:].rearrange("p b a n -> p (b a n)")
        turn_flat = turn_ps[:].rearrange("p b n -> p (b n)")
        g_ps = [[ring[d][:, G_FROM[d]:] for d in range(C)],
                [gram_flat[:, 0:D], gram_flat[:, D:2 * D - G_FROM[1]],
                 turn_flat[:, 0:D // 2], turn_flat[:, D // 2:]]]

        wl_loaded = [sem(f"wl_loaded{k}") for k in range(C)]
        wg_loaded, wv_loaded, wo_loaded = sem("wg_loaded"), sem("wv_loaded"), sem("wo_loaded")
        adj_loaded, gate_loaded, sigma_loaded = sem("adj_loaded"), sem("gate_loaded"), sem("sigma_loaded")
        ident_zeroed, ident_made, off_made = sem("ident_zeroed"), sem("ident_made"), sem("off_made")
        ones_made, mask_made = sem("ones_made"), sem("mask_made")
        gate_exp, sigma_exp, scalar_step = sem("gate_exp"), sem("sigma_exp"), sem("scalar_step")
        w_hi_made, w_lo_made = sem("w_hi_made"), sem("w_lo_made")
        g_made, u_hi_made, u_lo_made = sem("g_made"), sem("u_hi_made"), sem("u_lo_made")
        wot_made, wot_hi_made, wot_lo_made = sem("wot_made"), sem("wot_hi_made"), sem("wot_lo_made")
        wvo_made, wvo_hi_made, wvo_lo_made = sem("wvo_made"), sem("wvo_hi_made"), sem("wvo_lo_made")
        x_loaded = [[sem(f"x_loaded{i}_{b}") for b in range(GB)] for i in range(2)]
        y_stored = [sem(f"y_stored{b}") for b in range(GB)]
        xt_made, t_made, v_made, o_made = sem("xt_made"), sem("t_made"), sem("v_made"), sem("o_made")
        gram_made, turned = sem("gram_made"), sem("turned")
        xt_hi_made, xt_lo_made = sem("xt_hi_made"), sem("xt_lo_made")
        t_hi_made, t_lo_made = sem("t_hi_made"), sem("t_lo_made")
        v_hi_made, v_lo_made = sem("v_hi_made"), sem("v_lo_made")
        resid_made = sem("resid_made")
        pl_copied, diag_masked, diag_made, q_made = sem("pl_copied"), sem("diag_masked"), sem("diag_made"), sem("q_made")
        square_made, root_seed, root_step, root_made = sem("square_made"), sem("root_seed"), sem("root_step"), sem("root_made")
        s_made, mask_l_made, d_made, e_made = sem("s_made"), sem("mask_l_made"), sem("d_made"), sem("e_made")
        edges_l_made, edges_g_made, degree_made = sem("edges_l_made"), sem("edges_g_made"), sem("degree_made")
        scale_stored, scale_loaded = sem("scale_stored"), sem("scale_loaded")
        coef_step, coef_made = sem("coef_step"), sem("coef_made")
        scaled_made, k_made, kt_hi_made, kt_lo_made = sem("scaled_made"), sem("k_made"), sem("kt_hi_made"), sem("kt_lo_made")
        stats_made, ln_part_made, var_made = sem("stats_made"), sem("ln_part_made"), sem("var_made")
        ln_seed, ln_step = sem("ln_seed"), sem("ln_step")
        ln_ready, normed = sem("ln_ready"), sem("normed")

        def by_rows(w):
            return w.rearrange("(c p) d -> p c d", p=P)

        def x_loads(g, parity):
            return 16 + (g - parity) * 8

        NS = NEWTON * 4

        block = ctx.enter_context(nc.Block())

        @block.sync
        def _(sp):
            for k in range(C):
                sp.dma_start(wl_raw[:, k], w_lang[k * P:(k + 1) * P]).then_inc(wl_loaded[k], 16)
            sp.dma_start(wg_raw[:], by_rows(w_grav)).then_inc(wg_loaded, 16)
            for b in range(GB):
                sp.dma_start(x_nodes[0][:, b], x[b]).then_inc(x_loaded[0][b], 16)
            sp.dma_start(wo_raw[:], by_rows(w_o)).then_inc(wo_loaded, 16)
            sp.dma_start(wv_raw[:], by_rows(w_v)).then_inc(wv_loaded, 16)
            sp.dma_start(adj_sb[:], adj).then_inc(adj_loaded, 16)
            sp.dma_start(scalars[:, 0:1], gate_logit.partition_broadcast(P)).then_inc(gate_loaded, 16)
            sp.dma_start(scalars[:, 1:2], log_sigma.partition_broadcast(P)).then_inc(sigma_loaded, 16)
            for b in range(GB):
                sp.dma_start(x_nodes[1][:, b], x[GB + b]).then_inc(x_loaded[1][b], 16)

            x_pairs = x.rearrange("(i q b) n d -> i q b n d", q=2, b=GB)
            y_pairs = y.rearrange("(i q b) n d -> i q b n d", q=2, b=GB)

            def store(pair, parity):
                for b in range(GB):
                    sp.wait_ge(normed, GB * (2 * pair + parity) + b + 1)
                    sp.dma_start(y_pairs[pair, parity, b], y_nodes[:, b]).then_inc(y_stored[b], 16)

            with sp.Fori(0, NG // 2 - 1) as pair:
                for parity in range(2):
                    for b in range(GB):
                        sp.wait_ge(resid_made, GB * (2 * pair + parity) + b + 1)
                        sp.dma_start(x_nodes[parity][:, b], x_pairs[pair + 1, parity, b])\
                            .then_inc(x_loaded[parity][b], 16)
                    store(pair, parity)
            for parity in range(2):
                store(NG // 2 - 1, parity)
            for b in range(GB):
                sp.wait_ge(y_stored[b], 16 * NG)

        @block.tensor
        def _(pe):
            def product(out, pairs):
                for n, (lhsT, rhs) in enumerate(pairs):
                    last = nc.tensor.matmul(out, lhsT, rhs, start=(n == 0), stop=(n == len(pairs) - 1))
                return last

            def turn_x(g, parity, b):
                pe.wait_ge(x_loaded[parity][b], x_loads(g, parity))
                for c in range(C):
                    last = nc.tensor.transpose(xt_ps[:, c], x_nodes[parity][:, b, c * P:(c + 1) * P], ident[:])
                last.then_inc(xt_made, 1)

            def project(g, parity, t):
                e, a = PROJECT_ORDER[t]
                pairs = []
                for d in range(e + 1):
                    at = (ROW_START[d] + e - d) * P
                    hi, lo = u_hi[:, a, at:at + P], u_lo[:, a, at:at + P]
                    xh = xt_hi[parity][:, d].rearrange("p b n -> p (b n)")
                    xl = xt_lo[parity][:, d].rearrange("p b n -> p (b n)")
                    pairs += [(hi, xh), (hi, xl), (lo, xh)]
                product(ring[t % RING][:], pairs).then_inc(t_made, 1)

            def value(g, parity, b):
                pairs = []
                for c in range(C):
                    xh, xl = xt_hi[parity][:, c, b], xt_lo[parity][:, c, b]
                    pairs += [(xh, wvo_hi[:, c]), (xh, wvo_lo[:, c]), (xl, wvo_hi[:, c])]
                product(ring[b][:], pairs).then_inc(v_made, 1)

            def gram(g, parity, b):
                pairs = []
                for c in range(C):
                    xh, xl = xt_hi[parity][:, c, b], xt_lo[parity][:, c, b]
                    th = t_hi[:, c, b].rearrange("p a n -> p (a n)")
                    tl = t_lo[:, c, b].rearrange("p a n -> p (a n)")
                    pairs += [(xh, th), (xh, tl), (xl, th)]
                product(gram_ps[:, b].rearrange("p a n -> p (a n)"), pairs).then_inc(gram_made, 1)

            def aggregate(g, b):
                product(ring[b][:], [(kt_hi[:, b], v_hi[:, b]), (kt_hi[:, b], v_lo[:, b]),
                                     (kt_lo[:, b], v_hi[:, b])]).then_inc(o_made, 1)

            def turn(m):
                for b in range(GB):
                    last = nc.tensor.transpose(turn_ps[:, b], m[:, b], ident[:])
                last.then_inc(turned, 1)

            def projects(g, parity, after_setup=False):
                pe.wait_ge(xt_hi_made, GB * (g + 1))
                pe.wait_ge(xt_lo_made, GB * (g + 1))
                for t in range(NT):
                    if t >= RING:
                        pe.wait_ge(t_lo_made, NT * g + t - RING + 1)
                    elif after_setup:
                        pe.wait_ge(wot_lo_made, t + 1)
                    else:
                        pe.wait_ge(v_lo_made, GB * (g - 1) + t + 1)
                    if after_setup:
                        pe.wait_ge(u_lo_made, C * (PROJECT_ORDER[t][1] + 1))
                    project(g, parity, t)
                    yield t

            for k in range(C):
                pe.wait_ge(w_lo_made, k + 1)
                for d in range(C):
                    own = slice(d * P, (d + 1) * P)
                    for n, (lhs, rhs) in enumerate(((wl_hi, wl_hi), (wl_hi, wl_lo), (wl_lo, wl_hi))):
                        last = nc.tensor.matmul(g_ps[0][d], lhs[:, k, own], rhs[:, k, G_FROM[d]:],
                                                start=(k == 0 and n == 0), stop=(k == C - 1 and n == 2))
                    if k == C - 1:
                        last.then_inc(g_made, 1)

            def gram_of_grav(d):
                own = slice(d * P, (d + 1) * P)
                pairs = []
                for k in range(C):
                    pairs += [(lhs[:, k, own], rhs[:, k, G_FROM[d]:])
                              for lhs, rhs in ((wg_hi, wg_hi), (wg_hi, wg_lo), (wg_lo, wg_hi))]
                product(g_ps[1][d], pairs).then_inc(g_made, 1)

            def turn_wo(k):
                pe.wait_ge(u_lo_made, k + 1)
                for e in range(C):
                    last = nc.tensor.transpose(ring[k][:, e * P:(e + 1) * P], wo_raw[:, e, k * P:(k + 1) * P], ident[:])
                last.then_inc(wot_made, 1)

            pe.wait_ge(ident_made, 1)
            turn_x(0, 0, 0)
            pe.wait_ge(w_lo_made, 2 * C)
            for d in range(C):
                gram_of_grav(d)
                if d < C - 1:
                    pe.wait_ge(xt_lo_made, d + 1)
                    turn_x(0, 0, d + 1)
                if d == 1:
                    pe.wait_ge(wo_loaded, 16)
                if d in (1, 2):
                    turn_wo(2 * d - 2)
                    turn_wo(2 * d - 1)
            for _ in projects(0, 0, after_setup=True):
                pass
            pe.wait_ge(w_lo_made, 3 * C)
            for d in range(C):
                own = slice(d * P, (d + 1) * P)
                pairs = []
                for k in range(C):
                    pairs += [(lhs[:, k, own], rhs[:, k]) for lhs, rhs in ((wv_hi, wot_hi), (wv_hi, wot_lo), (wv_lo, wot_hi))]
                pe.wait_ge(t_lo_made, NT - RING + d + 1)
                product(ring[d][:], pairs).then_inc(wvo_made, 1)

            def iteration(g, parity, first=False, last=False):
                pe.wait_ge(t_hi_made, NT * (g + 1))
                pe.wait_ge(t_lo_made, NT * (g + 1))
                if not first:
                    pe.wait_ge(pl_copied, g)
                    pe.wait_ge(q_made, g)
                for b in range(GB):
                    gram(g, parity, b)
                for b in range(GB):
                    if not last:
                        pe.wait_ge(xt_lo_made, GB * (g + 1) + b)
                        turn_x(g + 1, 1 - parity, b)
                    if first:
                        if b == 0:
                            pe.wait_ge(wvo_lo_made, C)
                    else:
                        pe.wait_ge(resid_made, GB * (g - 1) + b + 1)
                    value(g, parity, b)
                    if b == 0:
                        pe.wait_ge(pl_copied, g + 1)
                        if not first:
                            pe.wait_ge(kt_lo_made, g)
                        turn(p_l)
                    if b == 1:
                        pe.wait_ge(q_made, g + 1)
                        pe.wait_ge(s_made, g + 1)
                        turn(q_g)

                def turn_k():
                    pe.wait_ge(k_made, g + 1)
                    pe.wait_ge(d_made, g + 1)
                    turn(k_sum)

                if last:
                    turn_k()
                else:
                    for t in projects(g + 1, 1 - parity):
                        if t == 5:
                            turn_k()
                pe.wait_ge(kt_hi_made, g + 1)
                pe.wait_ge(kt_lo_made, g + 1)
                for b in range(GB):
                    if last:
                        pe.wait_ge(v_lo_made, GB * g + b + 1)
                    else:
                        pe.wait_ge(t_lo_made, NT * (g + 1) + NT - RING + b + 1)
                    aggregate(g, b)

            iteration(0, 0, first=True)
            with pe.Fori(1, NG - 1, 2) as i:
                iteration(i, 1)
                iteration(i + 1, 0)
            iteration(NG - 1, 1, last=True)

        @block.scalar
        def _(act):
            def hi_of(out, in_):
                return nc.scalar.activation(out, in_, ACT.Copy)

            def split_x(g, parity, b):
                act.wait_ge(xt_made, GB * g + b + 1)
                hi_of(xt_hi[parity][:, :, b], xt_ps[:]).then_inc(xt_hi_made, 1)

            def split_t(g, t):
                e, a = PROJECT_ORDER[t]
                act.wait_ge(t_made, NT * g + t + 1)
                hi_of(t_hi[:, e, :, a], ring[t % RING][:].rearrange("p (b n) -> p b n", b=GB)).then_inc(t_hi_made, 1)

            def split_v(g, b):
                act.wait_ge(v_made, GB * g + b + 1)
                hi_of(v_hi[:, b], ring[b][:]).then_inc(v_hi_made, 1)

            def split_w(hi, raw):
                for k in range(C):
                    if raw is wl_raw:
                        act.wait_ge(wl_loaded[k], 16)
                    hi_of(hi[:, k], raw[:, k]).then_inc(w_hi_made, 1)

            def split_u(a):
                for d in range(C):
                    act.wait_ge(g_made, C * a + (C if a and d == C - 2 else d + 1))
                    at, own, n = ROW_START[d] * P, d * P - G_FROM[d], (C - 1 - d) * P
                    if n:
                        hi_of(u_hi[:, a, at + P:at + P + n], g_ps[a][d][:, own + P:])
                    nc.scalar.activation(u_hi[:, a, at:at + P], g_ps[a][d][:, own:own + P], ACT.Copy, scale=0.5)\
                        .then_inc(u_hi_made, 1)

            def split_wot(k):
                act.wait_ge(wot_made, k + 1)
                hi_of(wot_hi[:, k], ring[k][:]).then_inc(wot_hi_made, 1)

            split_w(wl_hi, wl_raw)
            act.wait_ge(wg_loaded, 16)
            split_w(wg_hi, wg_raw)
            split_x(0, 0, 0)
            split_u(0)
            split_x(0, 0, 1)
            split_x(0, 0, 2)
            split_wot(0)
            split_wot(1)
            split_x(0, 0, 3)
            split_wot(2)
            split_wot(3)
            split_u(1)
            act.wait_ge(wv_loaded, 16)
            split_w(wv_hi, wv_raw)
            act.wait_ge(gate_loaded, 16)
            nc.scalar.activation(scalars[:, 2:3], scalars[:, 0:1], ACT.Exp, scale=-1.0).then_inc(gate_exp, 1)
            act.wait_ge(sigma_loaded, 16)
            nc.scalar.activation(scalars[:, 3:4], scalars[:, 1:2], ACT.Exp).then_inc(sigma_exp, 1)
            for t in range(NT):
                split_t(0, t)
            for d in range(C):
                act.wait_ge(wvo_made, d + 1)
                hi_of(wvo_hi[:, d], ring[d][:]).then_inc(wvo_hi_made, 1)

            def copy_pl(g):
                act.wait_ge(gram_made, GB * (g + 1))
                act.wait_ge(diag_masked, 2 * (g + 1))
                nc.scalar.activation(p_l[:], gram_ps[:, :, 0], ACT.Copy).then_inc(pl_copied, 1)

            def exp_g(g):
                act.wait_ge(d_made, g + 1)
                nc.scalar.activation(e_g[:], d_g[:], ACT.Exp, scale=scalars[:, 6:7]).then_inc(e_made, 1)

            def split_k(g):
                act.wait_ge(turned, 3 * (g + 1))
                hi_of(kt_hi[:], turn_ps[:]).then_inc(kt_hi_made, 1)

            def store_scale(g):
                act.wait_ge(root_step, NS * (g + 1))
                nc.scalar.dma_start(scale_dram.rearrange("b n -> n b"), row_scale[:, 0],
                                    allow_slow_non_contiguous=True).then_inc(scale_stored, 16)

            def load_scale(g):
                act.wait_ge(scale_stored, 16 * (g + 1))
                nc.scalar.dma_start(scale_rows[:].rearrange("p b n -> p (b n)"),
                                    scale_dram.rearrange("b n -> (b n)").partition_broadcast(P))\
                    .then_inc(scale_loaded, 16)

            def normalise(g, b):
                act.wait_ge(ln_ready, g + 1)
                nc.scalar.activation(y_nodes[:, b], y_nodes[:, b], ACT.Identity, scale=ln_root[:, 3, b:b + 1],
                                     bias=ln_bias[:, b:b + 1]).then_inc(normed, 1)

            def iteration(g, parity, first=False, last=False):
                copy_pl(g)
                for b in range(GB):
                    if not last:
                        split_x(g + 1, 1 - parity, b)
                    if b == 2:
                        exp_g(g)
                    split_v(g, b)
                    if not first:
                        normalise(g - 1, b)
                    if b == 1:
                        store_scale(g)
                    if b == 2:
                        load_scale(g)
                if last:
                    split_k(g)
                else:
                    for t in range(NT):
                        split_t(g + 1, t)
                        if t == 5:
                            split_k(g)

            act.wait_ge(scalar_step, 4)
            iteration(0, 0, first=True)
            with act.Fori(1, NG - 1, 2) as i:
                iteration(i, 1)
                iteration(i + 1, 0)
            iteration(NG - 1, 1, last=True)
            for b in range(GB):
                normalise(NG - 1, b)

        @block.vector
        def _(dve):
            def lo_of(out, whole, hi):
                return nc.vector.tensor_tensor(out, whole, hi.bitcast(F32), ALU.subtract)

            def split_x(g, parity, b):
                dve.wait_ge(xt_hi_made, GB * g + b + 1)
                lo_of(xt_lo[parity][:, :, b], xt_ps[:], xt_hi[parity][:, :, b]).then_inc(xt_lo_made, 1)

            def split_t(g, t):
                e, a = PROJECT_ORDER[t]
                dve.wait_ge(t_hi_made, NT * g + t + 1)
                lo_of(t_lo[:, e, :, a], ring[t % RING][:].rearrange("p (b n) -> p b n", b=GB), t_hi[:, e, :, a])\
                    .then_inc(t_lo_made, 1)

            def split_v(g, b):
                dve.wait_ge(v_hi_made, GB * g + b + 1)
                lo_of(v_lo[:, b], ring[b][:], v_hi[:, b]).then_inc(v_lo_made, 1)

            def over_nodes(v):
                return v.unsqueeze(2).broadcast_to([P, GB, N])

            def split_w(first, raw, hi, lo):
                for k in range(C):
                    dve.wait_ge(w_hi_made, first + k + 1)
                    lo_of(lo[:, k], raw[:, k], hi[:, k]).then_inc(w_lo_made, 1)

            def split_u(a):
                for d in range(C):
                    dve.wait_ge(u_hi_made, C * a + (C if a and d == C - 2 else d + 1))
                    at, own, n = ROW_START[d] * P, d * P - G_FROM[d], (C - 1 - d) * P
                    if n:
                        lo_of(u_lo[:, a, at + P:at + P + n], g_ps[a][d][:, own + P:], u_hi[:, a, at + P:at + P + n])
                    nc.vector.scalar_tensor_tensor(out=u_lo[:, a, at:at + P], in0=g_ps[a][d][:, own:own + P],
                                                   scalar=0.5, in1=u_hi[:, a, at:at + P].bitcast(F32),
                                                   op0=ALU.mult, op1=ALU.subtract).then_inc(u_lo_made, 1)

            def split_wot(k):
                dve.wait_ge(wot_hi_made, k + 1)
                lo_of(wot_lo[:, k], ring[k][:], wot_hi[:, k]).then_inc(wot_lo_made, 1)

            split_w(0, wl_raw, wl_hi, wl_lo)
            split_w(C, wg_raw, wg_hi, wg_lo)
            split_x(0, 0, 0)
            split_u(0)
            split_x(0, 0, 1)
            split_x(0, 0, 2)
            split_wot(0)
            split_wot(1)
            split_x(0, 0, 3)
            split_wot(2)
            split_wot(3)
            split_u(1)
            split_w(2 * C, wv_raw, wv_hi, wv_lo)
            nc.vector.memset(row_scale[:, 1], 1.0).then_inc(ones_made, 1)
            nc.vector.memset(three_halves[:], 1.5).then_inc(ones_made, 1)
            dve.wait_ge(gate_exp, 1)
            dve.wait_ge(sigma_exp, 1)
            nc.vector.tensor_scalar(scalars[:, 4:5], scalars[:, 2:3], 1.0, None, ALU.add).then_inc(scalar_step, 1)
            nc.vector.tensor_tensor(scalars[:, 5:6], scalars[:, 3:4], scalars[:, 3:4], ALU.mult).then_inc(scalar_step, 1)
            dve.wait_ge(scalar_step, 2)
            nc.vector.reciprocal(scalars[:, 7:8], scalars[:, 4:5]).then_inc(scalar_step, 1)
            nc.vector.reciprocal(scalars[:, 6:7], scalars[:, 5:6]).then_inc(scalar_step, 1)
            dve.wait_ge(scalar_step, 4)
            dve.wait_ge(ones_made, 2)
            nc.vector.tensor_scalar(mix[:, 0], row_scale[:, 1], scalars[:, 7:8], None, ALU.mult).then_inc(scalar_step, 1)
            dve.wait_ge(scalar_step, 5)
            nc.vector.tensor_scalar(mix[:, 1], mix[:, 0], -1.0, 1.0, ALU.mult, ALU.add).then_inc(scalar_step, 1)
            dve.wait_ge(adj_loaded, 16)
            dve.wait_ge(ident_made, 1)
            nc.vector.tensor_scalar(off_diag[:], ident[:], -1.0, 1.0, ALU.mult, ALU.add).then_inc(off_made, 1)
            dve.wait_ge(off_made, 1)
            nc.vector.tensor_tensor(mask[:], adj_sb[:], off_diag[:], ALU.mult).then_inc(mask_made, 1)

            for t in range(NT):
                split_t(0, t)
            for d in range(C):
                dve.wait_ge(wvo_hi_made, d + 1)
                lo_of(wvo_lo[:, d], ring[d][:], wvo_hi[:, d]).then_inc(wvo_lo_made, 1)

            def mask_diagonal(g):
                for half in range(2):
                    graphs = slice(2 * half, 2 * half + 2)
                    dve.wait_ge(gram_made, GB * g + 2 * half + 2)
                    nc.vector.tensor_tensor(p_diag[:, graphs].rearrange("p b a n -> p (b a) n"),
                                            gram_ps[:, graphs].rearrange("p b a n -> p (b a) n"),
                                            ident[:].unsqueeze(1).broadcast_to([P, 2 * A, N]), ALU.mult)\
                        .then_inc(diag_masked, 1)

            def diagonal(g):
                dve.wait_ge(diag_masked, 2 * (g + 1))
                nc.vector.tensor_reduce(diag[:], p_diag[:], AX_X, ALU.add).then_inc(diag_made, 1)
                dve.wait_ge(diag_made, g + 1)
                nc.vector.tensor_scalar(square[:], diag[:, :, 0], 2.0, EPS * EPS, ALU.mult, ALU.max)\
                    .then_inc(square_made, 1)
                dve.wait_ge(square_made, g + 1)
                nc.vector.tensor_scalar(square_half[:], square[:], -0.5, None, ALU.mult)
                nc.vector.tensor_scalar(root[:, 0].bitcast(I32), square[:].bitcast(I32), -0.5, ROOT_MAGIC,
                                        ALU.mult, ALU.add).then_inc(root_seed, 1)

            def make_q(g):
                dve.wait_ge(pl_copied, g + 1)
                nc.vector.tensor_tensor(q_g[:], gram_ps[:, :, 1], over_nodes(diag[:, :, 1]), ALU.subtract)\
                    .then_inc(q_made, 1)

            def add_s(g):
                dve.wait_ge(turned, 3 * g + 1)
                nc.vector.tensor_tensor(s_l[:], turn_ps[:], p_l[:], ALU.add).then_inc(s_made, 1)

            def add_d(g):
                dve.wait_ge(turned, 3 * g + 2)
                nc.vector.tensor_tensor(d_g[:], turn_ps[:], q_g[:], ALU.add).then_inc(d_made, 1)

            def edges_g(g):
                dve.wait_ge(e_made, g + 1)
                nc.vector.scalar_tensor_tensor(out=edges[:, 1], in0=e_g[:], scalar=1.0,
                                               in1=mask[:].unsqueeze(1).broadcast_to([P, GB, N]),
                                               op0=ALU.min, op1=ALU.mult).then_inc(edges_g_made, 1)

            def mask_l(g):
                dve.wait_ge(s_made, g + 1)
                nc.vector.scalar_tensor_tensor(out=m_l[:], in0=s_l[:], scalar=0.0,
                                               in1=mask[:].unsqueeze(1).broadcast_to([P, GB, N]),
                                               op0=ALU.max, op1=ALU.mult).then_inc(mask_l_made, 1)

            def coefficients(g):
                step = 4 * g
                dve.wait_ge(edges_g_made, g + 1)
                dve.wait_ge(edges_l_made, g + 1)
                nc.vector.tensor_reduce(degree[:], edges[:], AX_X, ALU.add).then_inc(degree_made, 1)
                dve.wait_ge(degree_made, g + 1)
                nc.vector.tensor_tensor(coef[:, 0], degree[:], row_scale[:], ALU.mult).then_inc(coef_step, 1)
                dve.wait_ge(coef_step, step + 1)
                nc.vector.tensor_scalar(coef[:, 1], coef[:, 0], EPS, None, ALU.max).then_inc(coef_step, 1)
                dve.wait_ge(coef_step, step + 2)
                nc.vector.reciprocal(coef[:, 0], coef[:, 1]).then_inc(coef_step, 1)
                dve.wait_ge(coef_step, step + 3)
                nc.vector.tensor_tensor(coef[:, 1], coef[:, 0], row_scale[:], ALU.mult).then_inc(coef_step, 1)
                dve.wait_ge(coef_step, step + 4)
                nc.vector.tensor_tensor(coef[:, 2], coef[:, 1], mix[:], ALU.mult).then_inc(coef_made, 1)

            def sum_k(g):
                dve.wait_ge(scaled_made, g + 1)
                nc.vector.tensor_tensor(k_sum[:], edges[:, 0], edges[:, 1], ALU.add).then_inc(k_made, 1)

            def split_k(g):
                dve.wait_ge(kt_hi_made, g + 1)
                lo_of(kt_lo[:], turn_ps[:], kt_hi[:]).then_inc(kt_lo_made, 1)

            def residual(g, parity, first):
                for b in range(GB):
                    dve.wait_ge(o_made, GB * g + b + 1)
                    if not first:
                        dve.wait_ge(y_stored[b], 16 * g)
                    nc.vector.tensor_tensor(y_nodes[:, b], ring[b][:], x_nodes[parity][:, b], ALU.add)\
                        .then_inc(resid_made, 1)
                    if b:
                        dve.wait_ge(resid_made, GB * g + b)
                        nc.vector.bn_stats(stats[:, b - 1], y_nodes[:, b - 1]).then_inc(stats_made, 1)
                dve.wait_ge(resid_made, GB * (g + 1))
                nc.vector.bn_stats(stats[:, GB - 1], y_nodes[:, GB - 1]).then_inc(stats_made, 1)
                dve.wait_ge(stats_made, GB * (g + 1))
                step = 5 * g
                nc.vector.tensor_tensor(ln_part[:, 0], stats[:, :, 1], stats[:, :, 4], ALU.add).then_inc(ln_part_made, 1)
                nc.vector.tensor_tensor(ln_part[:, 1], stats[:, :, 1], stats[:, :, 4], ALU.subtract)\
                    .then_inc(ln_part_made, 1)
                nc.vector.tensor_tensor(ln_part[:, 2], stats[:, :, 2], stats[:, :, 5], ALU.add).then_inc(ln_part_made, 1)
                dve.wait_ge(ln_part_made, step + 3)
                nc.vector.tensor_tensor(ln_part[:, 3], ln_part[:, 1], ln_part[:, 1], ALU.mult).then_inc(ln_part_made, 1)
                nc.vector.tensor_scalar(ln_part[:, 4], ln_part[:, 2], 1.0 / D, LN_EPS, ALU.mult, ALU.add)\
                    .then_inc(ln_part_made, 1)
                nc.vector.tensor_scalar(ln_mean[:], ln_part[:, 0], -0.5, None, ALU.mult)
                dve.wait_ge(ln_part_made, step + 5)
                nc.vector.scalar_tensor_tensor(out=ln_var[:], in0=ln_part[:, 3], scalar=0.25, in1=ln_part[:, 4],
                                               op0=ALU.mult, op1=ALU.add).then_inc(var_made, 1)
                dve.wait_ge(var_made, g + 1)
                nc.vector.tensor_scalar(ln_var_half[:], ln_var[:], -0.5, None, ALU.mult)
                nc.vector.tensor_scalar(ln_root[:, 0].bitcast(I32), ln_var[:].bitcast(I32), -0.5, ROOT_MAGIC,
                                        ALU.mult, ALU.add).then_inc(ln_seed, 1)

            def iteration(g, parity, first=False, last=False):
                mask_diagonal(g)
                for b in range(GB):
                    if not last:
                        split_x(g + 1, 1 - parity, b)
                    if b == 0:
                        diagonal(g)
                        make_q(g)
                        add_s(g)
                    if b == 3:
                        edges_g(g)
                        if last:
                            coefficients(g)
                    split_v(g, b)
                    if b == 1:
                        add_d(g)
                        mask_l(g)
                if last:
                    sum_k(g)
                    split_k(g)
                else:
                    coefficients(g)
                    for t in range(NT):
                        split_t(g + 1, t)
                        if t == 2:
                            sum_k(g)
                        if t == 5:
                            split_k(g)
                residual(g, parity, first)

            dve.wait_ge(scalar_step, 6)
            dve.wait_ge(mask_made, 1)
            iteration(0, 0, first=True)
            with dve.Fori(1, NG - 1, 2) as i:
                iteration(i, 1)
                iteration(i + 1, 0)
            iteration(NG - 1, 1, last=True)

        @block.gpsimd
        def _(pool):
            nc.gpsimd.memset(ident[:], 0.0).then_inc(ident_zeroed, 1)
            pool.wait_ge(ident_zeroed, 1)
            nc.gpsimd.affine_select(out=ident[:], in_=ident[:], compare_op=ALU.not_equal, fill=1.0, base=0,
                                    pattern=[[-1, P]], channel_multiplier=1).then_inc(ident_made, 1)

            def inverse_root(value_half, guess, out, step, base):
                for n in range(NEWTON):
                    at = base + 4 * n
                    if n:
                        pool.wait_ge(step, at)
                    nc.gpsimd.tensor_tensor(guess[:, 1], guess[:, 0], guess[:, 0], ALU.mult).then_inc(step, 1)
                    pool.wait_ge(step, at + 1)
                    nc.gpsimd.tensor_tensor(guess[:, 2], guess[:, 1], value_half, ALU.mult).then_inc(step, 1)
                    pool.wait_ge(step, at + 2)
                    nc.gpsimd.tensor_tensor(guess[:, 1], guess[:, 2], three_halves[:], ALU.add).then_inc(step, 1)
                    pool.wait_ge(step, at + 3)
                    nc.gpsimd.tensor_tensor(out if n == NEWTON - 1 else guess[:, 0], guess[:, 0], guess[:, 1],
                                            ALU.mult).then_inc(step, 1)
                pool.wait_ge(step, base + NS)

            def layernorm_factors(g):
                pool.wait_ge(ln_seed, g + 1)
                inverse_root(ln_var_half[:], ln_root, ln_root[:, 3], ln_step, NS * g)
                nc.gpsimd.tensor_tensor(ln_bias[:], ln_mean[:], ln_root[:, 3], ALU.mult).then_inc(ln_ready, 1)

            def node_scale(g):
                pool.wait_ge(root_seed, g + 1)
                inverse_root(square_half[:], root, row_scale[:, 0], root_step, NS * g)

            def edges_l(g):
                pool.wait_ge(mask_l_made, g + 1)
                pool.wait_ge(scale_loaded, 16 * (g + 1))
                nc.gpsimd.tensor_tensor(edges[:, 0], m_l[:], scale_rows[:], ALU.mult).then_inc(edges_l_made, 1)

            def scale_edges(g):
                pool.wait_ge(coef_made, g + 1)
                nc.gpsimd.tensor_tensor(edges[:], edges[:], coef[:, 2].unsqueeze(3).broadcast_to([P, A, GB, N]),
                                        ALU.mult).then_inc(scaled_made, 1)

            pool.wait_ge(ones_made, 2)

            def iteration(g, first=False):
                if not first:
                    layernorm_factors(g - 1)
                node_scale(g)
                edges_l(g)
                scale_edges(g)

            iteration(0, first=True)
            with pool.Fori(1, NG - 1, 2) as i:
                iteration(i)
                iteration(i + 1)
            iteration(NG - 1)
            layernorm_factors(NG - 1)


_INS = ["x", "adj", "L0_gnn_W_lang", "L0_gnn_W_grav", "L0_gnn_W_V", "L0_gnn_W_O", "L0_gnn_gate_logit",
        "L0_gnn_log_sigma"]


def kernel(**inputs):
    import numpy as _np
    import concourse.bacc as _bacc
    from concourse.bass_utils import run_bass_kernel_spmd as _run

    nc = _bacc.Bacc("TRN2", target_bir_lowering=False, num_devices=1)
    arrays, args = {}, []
    for name in _INS:
        a = _np.ascontiguousarray(inputs[name])
        if a.ndim == 0:
            a = a.reshape(1)
        arrays[f"in_{name}"] = a
        args.append(nc.dram_tensor(f"in_{name}", a.shape, mybir.dt.from_np(a.dtype), kind="ExternalInput").ap())
    y = nc.dram_tensor("out_y", (B, N, D), F32, kind="ExternalOutput").ap()
    attention_layernorm(nc, *args, y)
    r = _run(nc, [arrays], core_ids=[0])
    return r.results[0]["out_y"]
```

```python
from contextlib import ExitStack

import concourse.bass as bass
from concourse import mybir

F32 = mybir.dt.float32
F32R = mybir.dt.float32r
I32 = mybir.dt.int32
ALU = mybir.AluOpType
ACT = mybir.ActivationFunctionType
AX_X = mybir.AxisListType.X

B, N, D = 128, 128, 512
P = 128
C = D // P
GB = 4
NG = B // GB
LAST = NG - 1
A = 2
RING = 4
EPS = 1e-8
LN_EPS = 1e-5
ROOT_MAGIC = float(0x5F3759DF)
NEWTON = 3
WARM_UP = 16

ROW_START = [sum(C - r for r in range(d)) for d in range(C)]
UBLOCKS = sum(C - d for d in range(C))
G_FROM = [min(d * P, D - 256) for d in range(C)]

PROJECT_ORDER = [(e, a) for a in range(A) for e in (3, 0, 2, 1)]
NT = len(PROJECT_ORDER)
NORMALISE_AFTER = {3: (0,), 5: (1,), 6: (2,), 7: (3,)}
GRAM_ORDER = [e for e, a in PROJECT_ORDER[:C]]
assert (GB + NT + GB) % RING == 0 and GB == RING


def attention_layernorm(nc, x, adj, w_lang, w_grav, w_v, w_o, gate_logit, log_sigma, y):
    with ExitStack() as ctx:
        def sb(name, shape, dt=F32):
            return ctx.enter_context(nc.sbuf_tensor(name, shape, dt))

        def psum(name, shape):
            return ctx.enter_context(nc.psum_tensor(name, shape, F32))

        def sem(name):
            return ctx.enter_context(nc.semaphore(name))

        u_hi = sb("u_hi", [P, A, UBLOCKS * P], F32R)
        u_lo = sb("u_lo", [P, A, UBLOCKS * P], F32R)
        wvo_hi = sb("wvo_hi", [P, C, D], F32R)
        wvo_lo = sb("wvo_lo", [P, C, D], F32R)
        x_nodes = [sb(f"x_nodes{i}", [P, GB, D]) for i in range(2)]
        xt_hi = [sb(f"xt_hi{i}", [P, C, GB, N], F32R) for i in range(2)]
        xt_lo = [sb(f"xt_lo{i}", [P, C, GB, N], F32R) for i in range(2)]
        t_hi = sb("t_hi", [P, C, GB, A, N], F32R)
        t_lo = sb("t_lo", [P, C, GB, A, N], F32R)
        v_hi = sb("v_hi", [P, GB, D], F32R)
        v_lo = sb("v_lo", [P, GB, D], F32R)
        p_diag = sb("p_diag", [P, GB, A, N])
        p_l = sb("p_l", [P, GB, N])
        q_g = sb("q_g", [P, GB, N])
        s_l = sb("s_l", [P, GB, N])
        m_l = sb("m_l", [P, GB, N])
        d_g = sb("d_g", [P, GB, N])
        e_g = sb("e_g", [P, GB, N])
        edges = sb("edges", [P, A, GB, N])
        kt_whole = sb("kt_whole", [P, GB, N])
        kt_hi = sb("kt_hi", [P, GB, N], F32R)
        kt_lo = sb("kt_lo", [P, GB, N], F32R)
        diag = sb("diag", [P, GB, A])
        square = sb("square", [P, GB])
        square_half = sb("square_half", [P, GB])
        root = sb("root", [P, 3, GB])
        degree = sb("degree", [P, A, GB])
        coef = sb("coef", [P, 3, A, GB])
        row_scale = sb("row_scale", [P, A, GB])
        stats = sb("stats", [P, GB, 6])
        ln_part = sb("ln_part", [P, 5, GB])
        ln_mean = sb("ln_mean", [P, GB])
        ln_var = sb("ln_var", [P, GB])
        ln_var_half = sb("ln_var_half", [P, GB])
        ln_root = sb("ln_root", [P, 4, GB])
        ln_bias = sb("ln_bias", [P, GB])
        ident = sb("ident", [P, P])
        off_diag = sb("off_diag", [P, P])
        adj_sb = sb("adj_sb", [P, N])
        mask = sb("mask", [P, N])
        mask_t = sb("mask_t", [P, N])
        scalars = sb("scalars", [P, 8])
        three_halves = sb("three_halves", [P, GB])
        mix = sb("mix", [P, A, GB])
        wl_raw, wg_raw, wv_raw, wo_raw = (sb(f"{n}_raw", [P, C, D]) for n in ("wl", "wg", "wv", "wo"))
        y_nodes = [sb("y_nodes", [P, GB, D])[:], wo_raw[:]]
        in_wl = wl_raw[:].rearrange("p c d -> p (c d)")
        in_wg = wg_raw[:].rearrange("p c d -> p (c d)")
        edges_t = in_wl[:, :A * GB * N].rearrange("p (a b n) -> p a b n", a=A, b=GB)
        coef_rows = in_wl[:, A * GB * N:2 * A * GB * N].rearrange("p (a b n) -> p a b n", a=A, b=GB)
        s_scaled = in_wg[:, :GB * N].rearrange("p (b n) -> p b n", b=GB)
        scale_rows = in_wg[:, GB * N:2 * GB * N].rearrange("p (b n) -> p b n", b=GB)
        scale_dram = nc.dram_tensor("scale_dram", (GB, N), F32).ap()
        coef_dram = nc.dram_tensor("coef_dram", (A * GB, N), F32).ap()

        def halves(t):
            flat = t[:].rearrange("p c b a n -> p (c b a n)")
            return tuple(flat[:, i * C * D:(i + 1) * C * D].rearrange("p (c d) -> p c d", c=C) for i in range(2))
        wl_hi, wl_lo = halves(t_hi)
        wg_hi, wg_lo = halves(t_lo)
        wot_hi, wot_lo = (t[1][:].rearrange("p c b n -> p c (b n)") for t in (xt_hi, xt_lo))
        wv_hi, wv_lo = v_hi, v_lo

        ring = [psum(f"ring{i}", [P, D]) for i in range(RING)]
        xt_ps = psum("xt_ps", [P, C, N])
        gram_ps = psum("gram_ps", [P, GB, A, N])
        turn_ps = psum("turn_ps", [P, GB, N])
        gram_flat = gram_ps[:].rearrange("p b a n -> p (b a n)")
        turn_flat = turn_ps[:].rearrange("p b n -> p (b n)")
        g_ps = [[ring[d][:, G_FROM[d]:] for d in range(C)],
                [gram_flat[:, 0:D], gram_flat[:, D:2 * D - G_FROM[1]],
                 turn_flat[:, 0:D // 2], turn_flat[:, D // 2:]]]

        wl_loaded = [sem(f"wl_loaded{k}") for k in range(C)]
        wg_loaded, wv_loaded, wo_loaded = sem("wg_loaded"), sem("wv_loaded"), sem("wo_loaded")
        adj_loaded, gate_loaded, sigma_loaded = sem("adj_loaded"), sem("gate_loaded"), sem("sigma_loaded")
        ident_zeroed, ident_made, off_made = sem("ident_zeroed"), sem("ident_made"), sem("off_made")
        ones_made, mask_made = sem("ones_made"), sem("mask_made")
        mask_turned, mask_t_made = sem("mask_turned"), sem("mask_t_made")
        gate_exp, sigma_exp, scalar_step = sem("gate_exp"), sem("sigma_exp"), sem("scalar_step")
        w_hi_made, w_lo_made = sem("w_hi_made"), sem("w_lo_made")
        g_made, u_hi_made, u_lo_made = sem("g_made"), sem("u_hi_made"), sem("u_lo_made")
        wot_made, wot_hi_made, wot_lo_made = sem("wot_made"), sem("wot_hi_made"), sem("wot_lo_made")
        wvo_made, wvo_hi_made, wvo_lo_made = sem("wvo_made"), sem("wvo_hi_made"), sem("wvo_lo_made")
        x_loaded = [[sem(f"x_loaded{i}_{b}") for b in range(GB)] for i in range(2)]
        y_stored = [sem(f"y_stored{b}") for b in range(GB)]
        xt_made, t_made, v_made, o_made = sem("xt_made"), sem("t_made"), sem("v_made"), sem("o_made")
        gram_made, turned = sem("gram_made"), sem("turned")
        xt_hi_made, xt_lo_made = sem("xt_hi_made"), sem("xt_lo_made")
        t_hi_made, t_lo_made = sem("t_hi_made"), sem("t_lo_made")
        v_hi_made, v_lo_made = sem("v_hi_made"), sem("v_lo_made")
        x_copied, resid_made = sem("x_copied"), sem("resid_made")
        pl_copied, diag_masked, diag_made, q_made = sem("pl_copied"), sem("diag_masked"), sem("diag_made"), sem("q_made")
        square_made, root_seed, root_step = sem("square_made"), sem("root_seed"), sem("root_step")
        s_made, mask_l_made, d_made, e_made = sem("s_made"), sem("mask_l_made"), sem("d_made"), sem("e_made")
        edges_l_made, edges_g_made, degree_made = sem("edges_l_made"), sem("edges_g_made"), sem("degree_made")
        scale_stored, scale_loaded = sem("scale_stored"), sem("scale_loaded")
        coef_step, coef_made = sem("coef_step"), sem("coef_made")
        coef_stored, coef_loaded = sem("coef_stored"), sem("coef_loaded")
        scaled_l_made = sem("scaled_l_made")
        s_scaled_made, edges_t_made = sem("s_scaled_made"), sem("edges_t_made")
        scaled_made, kt_made, kt_hi_made, kt_lo_made = sem("scaled_made"), sem("kt_made"), sem("kt_hi_made"), sem("kt_lo_made")
        stats_made, ln_part_made, var_made = sem("stats_made"), sem("ln_part_made"), sem("var_made")
        ln_seed, ln_step = sem("ln_seed"), sem("ln_step")
        ln_ready, normed, normed_last = sem("ln_ready"), sem("normed"), sem("normed_last")

        def by_rows(w):
            return w.rearrange("(c p) d -> p c d", p=P)

        def x_loads(g, parity):
            return 16 + (g - parity) * 8

        NS = NEWTON * 4

        block = ctx.enter_context(nc.Block())

        @block.sync
        def _(sp):
            for k in range(C):
                sp.dma_start(wl_raw[:, k], w_lang[k * P:(k + 1) * P]).then_inc(wl_loaded[k], 16)
            sp.dma_start(wg_raw[:], by_rows(w_grav)).then_inc(wg_loaded, 16)
            for b in range(GB):
                sp.dma_start(x_nodes[0][:, b], x[b]).then_inc(x_loaded[0][b], 16)
            sp.dma_start(wo_raw[:], by_rows(w_o)).then_inc(wo_loaded, 16)
            sp.dma_start(wv_raw[:], by_rows(w_v)).then_inc(wv_loaded, 16)
            sp.dma_start(adj_sb[:], adj).then_inc(adj_loaded, 16)
            sp.dma_start(scalars[:, 0:1], gate_logit.partition_broadcast(P)).then_inc(gate_loaded, 16)
            sp.dma_start(scalars[:, 1:2], log_sigma.partition_broadcast(P)).then_inc(sigma_loaded, 16)
            for b in range(GB):
                sp.dma_start(x_nodes[1][:, b], x[GB + b]).then_inc(x_loaded[1][b], 16)

            x_pairs = x.rearrange("(i q b) n d -> i q b n d", q=2, b=GB)
            y_pairs = y.rearrange("(i q b) n d -> i q b n d", q=2, b=GB)

            def store(g, parity, to):
                for b in range(GB):
                    sp.wait_ge(normed, GB * g + b + 1)
                    sp.dma_start(to[b], y_nodes[parity][:, b]).then_inc(y_stored[b], 16)

            def scale_to_rows(g):
                sp.wait_ge(root_step, NS * (g + 1))
                sp.dma_start(scale_dram.rearrange("b n -> n b"), row_scale[:, 0],
                             allow_slow_non_contiguous=True).then_inc(scale_stored, 16)
                sp.wait_ge(scale_stored, 16 * (g + 1))
                sp.dma_start(scale_rows.rearrange("p b n -> p (b n)"),
                             scale_dram.rearrange("b n -> (b n)").partition_broadcast(P)).then_inc(scale_loaded, 16)

            def coef_to_rows(g):
                sp.wait_ge(coef_made, g + 1)
                sp.dma_start(coef_dram.rearrange("v n -> n v"), coef[:, 2].rearrange("p a b -> p (a b)"),
                             allow_slow_non_contiguous=True).then_inc(coef_stored, 16)
                sp.wait_ge(coef_stored, 16 * (g + 1))
                sp.dma_start(coef_rows.rearrange("p a b n -> p (a b n)"),
                             coef_dram.rearrange("v n -> (v n)").partition_broadcast(P)).then_inc(coef_loaded, 16)

            def transfers(g, parity, y_before=None, x_after=None):
                if x_after is not None:
                    for b in range(GB):
                        sp.wait_ge(x_copied, GB * g + b + 1)
                        sp.dma_start(x_nodes[parity][:, b], x_after[b]).then_inc(x_loaded[parity][b], 16)
                if g is not LAST:
                    scale_to_rows(g)
                    coef_to_rows(g)
                if y_before is not None:
                    store(g - 1, 1 - parity, y_before)

            transfers(0, 0, x_after=x_pairs[1, 0])
            with sp.Fori(0, NG // 2 - 2) as pair:
                transfers(2 * pair + 1, 1, y_before=y_pairs[pair, 0], x_after=x_pairs[pair + 1, 1])
                transfers(2 * pair + 2, 0, y_before=y_pairs[pair, 1], x_after=x_pairs[pair + 2, 0])
            transfers(NG - 3, 1, y_before=y_pairs[NG // 2 - 2, 0], x_after=x_pairs[NG // 2 - 1, 1])
            transfers(NG - 2, 0, y_before=y_pairs[NG // 2 - 2, 1])
            transfers(LAST, 1, y_before=y_pairs[NG // 2 - 1, 0])
            for b in range(GB):
                if b == 0:
                    sp.wait_ge(normed, GB * LAST + 1)
                else:
                    sp.wait_ge(normed_last, b)
                sp.dma_start(y_pairs[NG // 2 - 1, 1, b], y_nodes[1][:, b]).then_inc(y_stored[b], 16)
            for b in range(GB):
                sp.wait_ge(y_stored[b], 16 * NG)

        @block.tensor
        def _(pe):
            def product(out, pairs):
                for n, (lhsT, rhs) in enumerate(pairs):
                    last = nc.tensor.matmul(out, lhsT, rhs, start=(n == 0), stop=(n == len(pairs) - 1))
                return last

            def turn_x(g, parity, b):
                pe.wait_ge(x_loaded[parity][b], x_loads(g, parity))
                for c in range(C):
                    last = nc.tensor.transpose(xt_ps[:, c], x_nodes[parity][:, b, c * P:(c + 1) * P], ident[:])
                last.then_inc(xt_made, 1)

            def project(g, parity, t):
                e, a = PROJECT_ORDER[t]
                pairs = []
                for d in range(e + 1):
                    at = (ROW_START[d] + e - d) * P
                    hi, lo = u_hi[:, a, at:at + P], u_lo[:, a, at:at + P]
                    xh = xt_hi[parity][:, d].rearrange("p b n -> p (b n)")
                    xl = xt_lo[parity][:, d].rearrange("p b n -> p (b n)")
                    pairs += [(hi, xh), (hi, xl), (lo, xh)]
                product(ring[t % RING][:], pairs).then_inc(t_made, 1)

            def value(g, parity, b, chunks=range(C)):
                for c in chunks:
                    xh, xl = xt_hi[parity][:, c, b], xt_lo[parity][:, c, b]
                    nc.tensor.matmul(ring[b][:], xh, wvo_hi[:, c], start=(c == 0), stop=False)
                    nc.tensor.matmul(ring[b][:], xh, wvo_lo[:, c], start=False, stop=False)
                    last = nc.tensor.matmul(ring[b][:], xl, wvo_hi[:, c], start=False, stop=(c == C - 1))
                if c == C - 1:
                    last.then_inc(v_made, 1)

            def gram(g, parity, b, chunks):
                out = gram_ps[:, b].rearrange("p a n -> p (a n)")
                for c in chunks:
                    xh, xl = xt_hi[parity][:, c, b], xt_lo[parity][:, c, b]
                    th = t_hi[:, c, b].rearrange("p a n -> p (a n)")
                    tl = t_lo[:, c, b].rearrange("p a n -> p (a n)")
                    nc.tensor.matmul(out, xh, th, start=(c == GRAM_ORDER[0]), stop=False)
                    nc.tensor.matmul(out, xh, tl, start=False, stop=False)
                    last = nc.tensor.matmul(out, xl, th, start=False, stop=(c == GRAM_ORDER[-1]))
                if c == GRAM_ORDER[-1]:
                    last.then_inc(gram_made, 1)

            def grams(g, parity):
                early, late = GRAM_ORDER[:-1], GRAM_ORDER[-1:]
                pe.wait_ge(t_hi_made, NT * (g + 1) - 1)
                pe.wait_ge(t_lo_made, NT * (g + 1) - 1)
                gram(g, parity, 0, early)
                gram(g, parity, 2, early)
                pe.wait_ge(t_hi_made, NT * (g + 1))
                pe.wait_ge(t_lo_made, NT * (g + 1))
                gram(g, parity, 0, late)
                gram(g, parity, 1, GRAM_ORDER)
                gram(g, parity, 2, late)
                gram(g, parity, 3, GRAM_ORDER)

            def aggregate(g, b):
                product(ring[b][:], [(kt_hi[:, b], v_hi[:, b]), (kt_hi[:, b], v_lo[:, b]),
                                     (kt_lo[:, b], v_hi[:, b])]).then_inc(o_made, 1)

            def turn(m, to):
                for b in range(GB):
                    last = nc.tensor.transpose(to[:, b], m[:, b], ident[:])
                last.then_inc(turned, 1)

            def projects(g, parity, after_setup=False):
                pe.wait_ge(xt_hi_made, GB * (g + 1))
                pe.wait_ge(xt_lo_made, GB * (g + 1))
                for t in range(NT):
                    if t >= RING:
                        pe.wait_ge(t_lo_made, NT * g + t - RING + 1)
                    elif after_setup:
                        pe.wait_ge(wot_lo_made, t + 1)
                    else:
                        pe.wait_ge(v_lo_made, GB * (g - 1) + t + 1)
                    if after_setup:
                        pe.wait_ge(u_lo_made, C * (PROJECT_ORDER[t][1] + 1))
                    project(g, parity, t)
                    yield t

            pe.wait_ge(ident_made, 1)
            for n in range(WARM_UP):
                nc.tensor.transpose(turn_ps[:, n % GB], ident[:], ident[:])

            for k in range(C):
                pe.wait_ge(w_lo_made, k + 1)
                for d in range(C):
                    own = slice(d * P, (d + 1) * P)
                    for n, (lhs, rhs) in enumerate(((wl_hi, wl_hi), (wl_hi, wl_lo), (wl_lo, wl_hi))):
                        last = nc.tensor.matmul(g_ps[0][d], lhs[:, k, own], rhs[:, k, G_FROM[d]:],
                                                start=(k == 0 and n == 0), stop=(k == C - 1 and n == 2))
                    if k == C - 1:
                        last.then_inc(g_made, 1)

            def gram_of_grav(d):
                own = slice(d * P, (d + 1) * P)
                pairs = []
                for k in range(C):
                    pairs += [(lhs[:, k, own], rhs[:, k, G_FROM[d]:])
                              for lhs, rhs in ((wg_hi, wg_hi), (wg_hi, wg_lo), (wg_lo, wg_hi))]
                product(g_ps[1][d], pairs).then_inc(g_made, 1)

            def turn_wo(k):
                pe.wait_ge(u_lo_made, k + 1)
                for e in range(C):
                    last = nc.tensor.transpose(ring[k][:, e * P:(e + 1) * P], wo_raw[:, e, k * P:(k + 1) * P], ident[:])
                last.then_inc(wot_made, 1)

            turn_x(0, 0, 0)
            pe.wait_ge(w_lo_made, 2 * C)
            for d in range(C):
                gram_of_grav(d)
                if d < C - 1:
                    pe.wait_ge(xt_lo_made, d + 1)
                    turn_x(0, 0, d + 1)
                if d == 1:
                    pe.wait_ge(wo_loaded, 16)
                if d in (1, 2):
                    turn_wo(2 * d - 2)
                    turn_wo(2 * d - 1)
            for _ in projects(0, 0, after_setup=True):
                pass
            pe.wait_ge(w_lo_made, 3 * C)
            for d in range(C):
                own = slice(d * P, (d + 1) * P)
                pairs = []
                for k in range(C):
                    pairs += [(lhs[:, k, own], rhs[:, k]) for lhs, rhs in ((wv_hi, wot_hi), (wv_hi, wot_lo), (wv_lo, wot_hi))]
                pe.wait_ge(t_lo_made, NT - RING + d + 1)
                product(ring[d][:], pairs).then_inc(wvo_made, 1)

            pe.wait_ge(mask_made, 1)
            nc.tensor.transpose(turn_ps[:, 0], mask[:], ident[:]).then_inc(mask_turned, 1)

            def aggregates(g, by_graph=False):
                pe.wait_ge(kt_hi_made, g + 1)
                pe.wait_ge(kt_lo_made, g + 1)
                for b in range(GB):
                    if by_graph:
                        pe.wait_ge(v_lo_made, GB * g + b + 1)
                    aggregate(g, b)

            def iteration(g, parity, first=False, last=False):
                if not last:
                    pe.wait_ge(xt_lo_made, GB * (g + 1))
                    turn_x(g + 1, 1 - parity, 0)
                if not first:
                    pe.wait_ge(pl_copied, g)
                    pe.wait_ge(q_made, g)
                grams(g, parity)
                if not first:
                    pe.wait_ge(v_lo_made, GB * g)
                    aggregates(g - 1)

                def turn_p():
                    pe.wait_ge(pl_copied, g + 1)
                    if first:
                        pe.wait_ge(mask_t_made, 1)
                    else:
                        pe.wait_ge(d_made, g)
                    turn(p_l, turn_ps)

                def turn_q():
                    pe.wait_ge(q_made, g + 1)
                    pe.wait_ge(s_made, g + 1)
                    turn(q_g, turn_ps)

                if not first:
                    turn_p()
                for b in range(GB):
                    if not last and b:
                        pe.wait_ge(xt_lo_made, GB * (g + 1) + b)
                        turn_x(g + 1, 1 - parity, b)
                    if first:
                        if b == 0:
                            pe.wait_ge(wvo_lo_made, C)
                    else:
                        pe.wait_ge(resid_made, GB * (g - 1) + b + 1)
                    if last and b in (1, GB - 1):
                        value(g, parity, b, range(0, C // 2))
                        if b == 1:
                            pe.wait_ge(s_scaled_made, g + 1)
                            turn(s_scaled, xt_ps)
                        else:
                            pe.wait_ge(kt_made, g + 1)
                            pe.wait_ge(d_made, g + 1)
                            turn(kt_whole, turn_ps)
                        value(g, parity, b, range(C // 2, C))
                    else:
                        value(g, parity, b)
                    if b == 0:
                        if first:
                            turn_p()
                        else:
                            turn_q()
                    if b == 1 and first:
                        turn_q()
                if last:
                    aggregates(g, by_graph=True)
                else:
                    for _ in projects(g + 1, 1 - parity):
                        pass

            iteration(0, 0, first=True)
            with pe.Fori(1, NG - 1, 2) as i:
                iteration(i, 1)
                iteration(i + 1, 0)
            iteration(NG - 1, 1, last=True)

        @block.scalar
        def _(act):
            def hi_of(out, in_):
                return nc.scalar.activation(out, in_, ACT.Copy)

            def split_x(g, parity, b):
                act.wait_ge(xt_made, GB * g + b + 1)
                hi_of(xt_hi[parity][:, :, b], xt_ps[:]).then_inc(xt_hi_made, 1)

            def split_t(g, t):
                e, a = PROJECT_ORDER[t]
                act.wait_ge(t_made, NT * g + t + 1)
                hi_of(t_hi[:, e, :, a], ring[t % RING][:].rearrange("p (b n) -> p b n", b=GB)).then_inc(t_hi_made, 1)

            def split_v(g, b):
                act.wait_ge(v_made, GB * g + b + 1)
                hi_of(v_hi[:, b], ring[b][:]).then_inc(v_hi_made, 1)

            def split_w(hi, raw):
                for k in range(C):
                    if raw is wl_raw:
                        act.wait_ge(wl_loaded[k], 16)
                    hi_of(hi[:, k], raw[:, k]).then_inc(w_hi_made, 1)

            def split_u(a):
                for d in range(C):
                    act.wait_ge(g_made, C * a + (C if a and d == C - 2 else d + 1))
                    at, own, n = ROW_START[d] * P, d * P - G_FROM[d], (C - 1 - d) * P
                    if n:
                        hi_of(u_hi[:, a, at + P:at + P + n], g_ps[a][d][:, own + P:])
                    nc.scalar.activation(u_hi[:, a, at:at + P], g_ps[a][d][:, own:own + P], ACT.Copy, scale=0.5)\
                        .then_inc(u_hi_made, 1)

            def split_wot(k):
                act.wait_ge(wot_made, k + 1)
                hi_of(wot_hi[:, k], ring[k][:]).then_inc(wot_hi_made, 1)

            split_w(wl_hi, wl_raw)
            act.wait_ge(wg_loaded, 16)
            split_w(wg_hi, wg_raw)
            split_x(0, 0, 0)
            split_u(0)
            split_x(0, 0, 1)
            split_x(0, 0, 2)
            split_wot(0)
            split_wot(1)
            split_x(0, 0, 3)
            split_wot(2)
            split_wot(3)
            split_u(1)
            for t in range(RING):
                split_t(0, t)
            act.wait_ge(wv_loaded, 16)
            split_w(wv_hi, wv_raw)
            act.wait_ge(gate_loaded, 16)
            nc.scalar.activation(scalars[:, 2:3], scalars[:, 0:1], ACT.Exp, scale=-1.0).then_inc(gate_exp, 1)
            act.wait_ge(sigma_loaded, 16)
            nc.scalar.activation(scalars[:, 3:4], scalars[:, 1:2], ACT.Exp).then_inc(sigma_exp, 1)
            for t in range(RING, NT):
                split_t(0, t)
            for d in range(C):
                act.wait_ge(wvo_made, d + 1)
                hi_of(wvo_hi[:, d], ring[d][:]).then_inc(wvo_hi_made, 1)

            def copy_pl(g):
                act.wait_ge(gram_made, GB * (g + 1))
                act.wait_ge(diag_masked, 2 * (g + 1))
                nc.scalar.activation(p_l[:], gram_ps[:, :, 0], ACT.Copy).then_inc(pl_copied, 1)

            def exp_g(g):
                act.wait_ge(d_made, g + 1)
                nc.scalar.activation(e_g[:], d_g[:], ACT.Exp, scale=scalars[:, 6:7]).then_inc(e_made, 1)

            def split_k(g, last=False):
                if last:
                    act.wait_ge(turned, 2 * g + 4)
                else:
                    act.wait_ge(kt_made, g + 1)
                hi_of(kt_hi[:], turn_ps[:] if last else kt_whole[:]).then_inc(kt_hi_made, 1)

            def normalise(g, parity, b):
                act.wait_ge(ln_ready, g + 1)
                nc.scalar.activation(y_nodes[parity][:, b], y_nodes[parity][:, b], ACT.Identity, scale=ln_root[:, 3, b:b + 1],
                                     bias=ln_bias[:, b:b + 1]).then_inc(normed, 1)

            def iteration(g, parity, first=False, last=False):
                if not last:
                    split_x(g + 1, 1 - parity, 0)
                if not first:
                    split_k(g - 1)
                copy_pl(g)
                for b in range(GB):
                    if not last and b:
                        split_x(g + 1, 1 - parity, b)
                    if b == 1 and last:
                        exp_g(g)
                    if b == 2 and not last:
                        exp_g(g)
                    if b == GB - 1 and last:
                        split_k(g, last=True)
                    split_v(g, b)
                if last:
                    for b in range(GB):
                        normalise(g - 1, 1 - parity, b)
                else:
                    for t in range(NT):
                        split_t(g + 1, t)
                        if t in NORMALISE_AFTER and not first:
                            for b in NORMALISE_AFTER[t]:
                                normalise(g - 1, 1 - parity, b)

            act.wait_ge(scalar_step, 4)
            iteration(0, 0, first=True)
            with act.Fori(1, NG - 1, 2) as i:
                iteration(i, 1)
                iteration(i + 1, 0)
            iteration(NG - 1, 1, last=True)
            normalise(LAST, 1, 0)

        @block.vector
        def _(dve):
            def lo_of(out, whole, hi):
                return nc.vector.tensor_tensor(out, whole, hi.bitcast(F32), ALU.subtract)

            def split_x(g, parity, b):
                dve.wait_ge(xt_hi_made, GB * g + b + 1)
                lo_of(xt_lo[parity][:, :, b], xt_ps[:], xt_hi[parity][:, :, b]).then_inc(xt_lo_made, 1)

            def split_t(g, t):
                e, a = PROJECT_ORDER[t]
                dve.wait_ge(t_hi_made, NT * g + t + 1)
                lo_of(t_lo[:, e, :, a], ring[t % RING][:].rearrange("p (b n) -> p b n", b=GB), t_hi[:, e, :, a])\
                    .then_inc(t_lo_made, 1)

            def split_v(g, b):
                dve.wait_ge(v_hi_made, GB * g + b + 1)
                lo_of(v_lo[:, b], ring[b][:], v_hi[:, b]).then_inc(v_lo_made, 1)

            def over_nodes(v):
                return v.unsqueeze(2).broadcast_to([P, GB, N])

            def split_w(first, raw, hi, lo):
                for k in range(C):
                    dve.wait_ge(w_hi_made, first + k + 1)
                    lo_of(lo[:, k], raw[:, k], hi[:, k]).then_inc(w_lo_made, 1)

            def split_u(a):
                for d in range(C):
                    dve.wait_ge(u_hi_made, C * a + (C if a and d == C - 2 else d + 1))
                    at, own, n = ROW_START[d] * P, d * P - G_FROM[d], (C - 1 - d) * P
                    if n:
                        lo_of(u_lo[:, a, at + P:at + P + n], g_ps[a][d][:, own + P:], u_hi[:, a, at + P:at + P + n])
                    nc.vector.scalar_tensor_tensor(out=u_lo[:, a, at:at + P], in0=g_ps[a][d][:, own:own + P],
                                                   scalar=0.5, in1=u_hi[:, a, at:at + P].bitcast(F32),
                                                   op0=ALU.mult, op1=ALU.subtract).then_inc(u_lo_made, 1)

            def split_wot(k):
                dve.wait_ge(wot_hi_made, k + 1)
                lo_of(wot_lo[:, k], ring[k][:], wot_hi[:, k]).then_inc(wot_lo_made, 1)

            split_w(0, wl_raw, wl_hi, wl_lo)
            split_w(C, wg_raw, wg_hi, wg_lo)
            split_x(0, 0, 0)
            split_u(0)
            split_x(0, 0, 1)
            split_x(0, 0, 2)
            split_wot(0)
            split_wot(1)
            split_x(0, 0, 3)
            split_wot(2)
            split_wot(3)
            split_u(1)
            for t in range(RING):
                split_t(0, t)
            split_w(2 * C, wv_raw, wv_hi, wv_lo)
            nc.vector.memset(row_scale[:, 1], 1.0).then_inc(ones_made, 1)
            nc.vector.memset(three_halves[:], 1.5).then_inc(ones_made, 1)
            dve.wait_ge(gate_exp, 1)
            dve.wait_ge(sigma_exp, 1)
            nc.vector.tensor_scalar(scalars[:, 4:5], scalars[:, 2:3], 1.0, None, ALU.add).then_inc(scalar_step, 1)
            nc.vector.tensor_tensor(scalars[:, 5:6], scalars[:, 3:4], scalars[:, 3:4], ALU.mult).then_inc(scalar_step, 1)
            dve.wait_ge(scalar_step, 2)
            nc.vector.reciprocal(scalars[:, 7:8], scalars[:, 4:5]).then_inc(scalar_step, 1)
            nc.vector.reciprocal(scalars[:, 6:7], scalars[:, 5:6]).then_inc(scalar_step, 1)
            dve.wait_ge(scalar_step, 4)
            dve.wait_ge(ones_made, 2)
            nc.vector.tensor_scalar(mix[:, 0], row_scale[:, 1], scalars[:, 7:8], None, ALU.mult).then_inc(scalar_step, 1)
            dve.wait_ge(scalar_step, 5)
            nc.vector.tensor_scalar(mix[:, 1], mix[:, 0], -1.0, 1.0, ALU.mult, ALU.add).then_inc(scalar_step, 1)
            dve.wait_ge(adj_loaded, 16)
            dve.wait_ge(ident_made, 1)
            nc.vector.tensor_scalar(off_diag[:], ident[:], -1.0, 1.0, ALU.mult, ALU.add).then_inc(off_made, 1)
            dve.wait_ge(off_made, 1)
            nc.vector.tensor_tensor(mask[:], adj_sb[:], off_diag[:], ALU.mult).then_inc(mask_made, 1)

            for t in range(RING, NT):
                split_t(0, t)
            for d in range(C):
                dve.wait_ge(wvo_hi_made, d + 1)
                lo_of(wvo_lo[:, d], ring[d][:], wvo_hi[:, d]).then_inc(wvo_lo_made, 1)
            dve.wait_ge(mask_turned, 1)
            nc.vector.tensor_copy(mask_t[:], turn_ps[:, 0]).then_inc(mask_t_made, 1)

            def mask_diagonal(g, half):
                graphs = slice(2 * half, 2 * half + 2)
                dve.wait_ge(gram_made, GB * g + 2 * half + 2)
                nc.vector.tensor_tensor(p_diag[:, graphs].rearrange("p b a n -> p (b a) n"),
                                        gram_ps[:, graphs].rearrange("p b a n -> p (b a) n"),
                                        ident[:].unsqueeze(1).broadcast_to([P, 2 * A, N]), ALU.mult)\
                    .then_inc(diag_masked, 1)

            def diagonal(g):
                dve.wait_ge(diag_masked, 2 * (g + 1))
                nc.vector.tensor_reduce(diag[:], p_diag[:], AX_X, ALU.add).then_inc(diag_made, 1)
                dve.wait_ge(diag_made, g + 1)
                nc.vector.tensor_scalar(square[:], diag[:, :, 0], 2.0, EPS * EPS, ALU.mult, ALU.max)\
                    .then_inc(square_made, 1)
                dve.wait_ge(square_made, g + 1)
                nc.vector.tensor_scalar(square_half[:], square[:], -0.5, None, ALU.mult)
                nc.vector.tensor_scalar(root[:, 0].bitcast(I32), square[:].bitcast(I32), -0.5, ROOT_MAGIC,
                                        ALU.mult, ALU.add).then_inc(root_seed, 1)

            def make_q(g):
                dve.wait_ge(pl_copied, g + 1)
                nc.vector.tensor_tensor(q_g[:], gram_ps[:, :, 1], over_nodes(diag[:, :, 1]), ALU.subtract)\
                    .then_inc(q_made, 1)

            def add_s(g):
                dve.wait_ge(turned, 2 * g + 1)
                nc.vector.tensor_tensor(s_l[:], turn_ps[:], p_l[:], ALU.add).then_inc(s_made, 1)

            def add_d(g):
                dve.wait_ge(turned, 2 * g + 2)
                nc.vector.tensor_tensor(d_g[:], turn_ps[:], q_g[:], ALU.add).then_inc(d_made, 1)

            def edges_g(g):
                dve.wait_ge(e_made, g + 1)
                nc.vector.scalar_tensor_tensor(out=edges[:, 1], in0=e_g[:], scalar=1.0,
                                               in1=mask[:].unsqueeze(1).broadcast_to([P, GB, N]),
                                               op0=ALU.min, op1=ALU.mult).then_inc(edges_g_made, 1)

            def mask_l(g):
                dve.wait_ge(s_made, g + 1)
                nc.vector.scalar_tensor_tensor(out=m_l[:], in0=s_l[:], scalar=0.0,
                                               in1=mask[:].unsqueeze(1).broadcast_to([P, GB, N]),
                                               op0=ALU.max, op1=ALU.mult).then_inc(mask_l_made, 1)

            def edges_l_last(g):
                dve.wait_ge(turned, 2 * g + 3)
                nc.vector.scalar_tensor_tensor(out=edges[:, 0], in0=xt_ps[:], scalar=0.0,
                                               in1=mask[:].unsqueeze(1).broadcast_to([P, GB, N]),
                                               op0=ALU.max, op1=ALU.mult).then_inc(edges_l_made, 1)

            def edges_lt(g):
                dve.wait_ge(s_scaled_made, g + 1)
                nc.vector.scalar_tensor_tensor(out=edges_t[:, 0], in0=s_scaled, scalar=0.0,
                                               in1=mask_t[:].unsqueeze(1).broadcast_to([P, GB, N]),
                                               op0=ALU.max, op1=ALU.mult).then_inc(edges_t_made, 1)

            def edges_gt(g):
                nc.vector.scalar_tensor_tensor(out=edges_t[:, 1], in0=e_g[:], scalar=1.0,
                                               in1=mask_t[:].unsqueeze(1).broadcast_to([P, GB, N]),
                                               op0=ALU.min, op1=ALU.mult).then_inc(edges_t_made, 1)

            def coefficients(g):
                step = 4 * g
                dve.wait_ge(edges_g_made, g + 1)
                dve.wait_ge(edges_l_made, g + 1)
                nc.vector.tensor_reduce(degree[:], edges[:], AX_X, ALU.add).then_inc(degree_made, 1)
                dve.wait_ge(degree_made, g + 1)
                nc.vector.tensor_tensor(coef[:, 0], degree[:], row_scale[:], ALU.mult).then_inc(coef_step, 1)
                dve.wait_ge(coef_step, step + 1)
                nc.vector.tensor_scalar(coef[:, 1], coef[:, 0], EPS, None, ALU.max).then_inc(coef_step, 1)
                dve.wait_ge(coef_step, step + 2)
                nc.vector.reciprocal(coef[:, 0], coef[:, 1]).then_inc(coef_step, 1)
                dve.wait_ge(coef_step, step + 3)
                nc.vector.tensor_tensor(coef[:, 1], coef[:, 0], row_scale[:], ALU.mult).then_inc(coef_step, 1)
                dve.wait_ge(coef_step, step + 4)
                nc.vector.tensor_tensor(coef[:, 2], coef[:, 1], mix[:], ALU.mult).then_inc(coef_made, 1)

            def sum_k(g):
                dve.wait_ge(scaled_made, g + 1)
                nc.vector.tensor_tensor(kt_whole[:], edges_t[:, 0], edges_t[:, 1], ALU.add).then_inc(kt_made, 1)

            def scale_last(g):
                dve.wait_ge(coef_made, g + 1)
                nc.vector.tensor_tensor(edges[:, 0], edges[:, 0], over_nodes(coef[:, 2, 0]), ALU.mult)\
                    .then_inc(scaled_l_made, 1)

            def sum_k_last(g):
                dve.wait_ge(scaled_l_made, 1)
                dve.wait_ge(scaled_made, g + 1)
                nc.vector.tensor_tensor(kt_whole[:], edges[:, 0], edges[:, 1], ALU.add).then_inc(kt_made, 1)

            def split_k(g, last=False):
                dve.wait_ge(kt_hi_made, g + 1)
                lo_of(kt_lo[:], turn_ps[:] if last else kt_whole[:], kt_hi[:]).then_inc(kt_lo_made, 1)

            def residual(g, parity, b):
                dve.wait_ge(o_made, GB * g + b + 1)
                dve.wait_ge(x_copied, GB * g + b + 1)
                nc.vector.tensor_tensor(y_nodes[parity][:, b], ring[b][:], y_nodes[parity][:, b], ALU.add)\
                    .then_inc(resid_made, 1)

            def bn(g, parity, b):
                dve.wait_ge(resid_made, GB * g + b + 1)
                nc.vector.bn_stats(stats[:, b], y_nodes[parity][:, b]).then_inc(stats_made, 1)

            def layernorm_start(g):
                dve.wait_ge(stats_made, GB * (g + 1))
                step = 5 * g
                nc.vector.tensor_tensor(ln_part[:, 0], stats[:, :, 1], stats[:, :, 4], ALU.add).then_inc(ln_part_made, 1)
                nc.vector.tensor_tensor(ln_part[:, 1], stats[:, :, 1], stats[:, :, 4], ALU.subtract)\
                    .then_inc(ln_part_made, 1)
                nc.vector.tensor_tensor(ln_part[:, 2], stats[:, :, 2], stats[:, :, 5], ALU.add).then_inc(ln_part_made, 1)
                dve.wait_ge(ln_part_made, step + 3)
                nc.vector.tensor_tensor(ln_part[:, 3], ln_part[:, 1], ln_part[:, 1], ALU.mult).then_inc(ln_part_made, 1)
                nc.vector.tensor_scalar(ln_part[:, 4], ln_part[:, 2], 1.0 / D, LN_EPS, ALU.mult, ALU.add)\
                    .then_inc(ln_part_made, 1)
                nc.vector.tensor_scalar(ln_mean[:], ln_part[:, 0], -0.5, None, ALU.mult)
                dve.wait_ge(ln_part_made, step + 5)
                nc.vector.scalar_tensor_tensor(out=ln_var[:], in0=ln_part[:, 3], scalar=0.25, in1=ln_part[:, 4],
                                               op0=ALU.mult, op1=ALU.add).then_inc(var_made, 1)
                dve.wait_ge(var_made, g + 1)
                nc.vector.tensor_scalar(ln_var_half[:], ln_var[:], -0.5, None, ALU.mult)
                nc.vector.tensor_scalar(ln_root[:, 0].bitcast(I32), ln_var[:].bitcast(I32), -0.5, ROOT_MAGIC,
                                        ALU.mult, ALU.add).then_inc(ln_seed, 1)

            def iteration(g, parity, first=False):
                before = None if first else (g - 1, 1 - parity)
                split_x(g + 1, 1 - parity, 0)
                if before:
                    split_k(g - 1)
                mask_diagonal(g, 0)
                mask_diagonal(g, 1)
                if before:
                    residual(*before, 0)
                diagonal(g)
                if before:
                    residual(*before, 1)
                make_q(g)
                add_s(g)
                if before:
                    residual(*before, 2)
                split_v(g, 0)
                split_x(g + 1, 1 - parity, 1)
                add_d(g)
                if before:
                    residual(*before, 3)
                mask_l(g)
                split_v(g, 1)
                edges_lt(g)
                split_x(g + 1, 1 - parity, 2)
                if before:
                    bn(*before, 0)
                    bn(*before, 1)
                edges_g(g)
                split_v(g, 2)
                split_x(g + 1, 1 - parity, 3)
                coefficients(g)
                split_v(g, 3)
                if before:
                    bn(*before, 2)
                    bn(*before, 3)
                    layernorm_start(*before[:1])
                for t in range(NT):
                    split_t(g + 1, t)
                    if t == 1:
                        edges_gt(g)
                sum_k(g)

            def last_iteration(g, parity):
                before = (g - 1, 1 - parity)
                split_k(g - 1)
                mask_diagonal(g, 0)
                mask_diagonal(g, 1)
                residual(*before, 0)
                diagonal(g)
                make_q(g)
                residual(*before, 1)
                add_s(g)
                residual(*before, 2)
                residual(*before, 3)
                bn(*before, 0)
                split_v(g, 0)
                add_d(g)
                bn(*before, 1)
                edges_l_last(g)
                edges_g(g)
                coefficients(g)
                scale_last(g)
                bn(*before, 2)
                sum_k_last(g)
                split_v(g, 1)
                split_v(g, 2)
                split_k(g, last=True)
                split_v(g, 3)
                bn(*before, 3)
                layernorm_start(*before[:1])
                for b in range(GB):
                    residual(g, parity, b)
                    if b:
                        bn(g, parity, b - 1)
                bn(g, parity, GB - 1)
                dve.wait_ge(ln_ready, g)
                layernorm_start(g)
                dve.wait_ge(ln_seed, g + 1)
                for n in range(NEWTON):
                    at = NS * g + 3 * n
                    if n:
                        dve.wait_ge(ln_step, at)
                    nc.vector.tensor_tensor(ln_root[:, 1], ln_root[:, 0], ln_root[:, 0], ALU.mult).then_inc(ln_step, 1)
                    dve.wait_ge(ln_step, at + 1)
                    nc.vector.tensor_tensor(ln_root[:, 2], ln_root[:, 1], ln_var_half[:], ALU.mult).then_inc(ln_step, 1)
                    dve.wait_ge(ln_step, at + 2)
                    if n == NEWTON - 1:
                        dve.wait_ge(normed, GB * g)
                    nc.vector.scalar_tensor_tensor(out=ln_root[:, 3 if n == NEWTON - 1 else 0], in0=ln_root[:, 2],
                                                   scalar=1.5, in1=ln_root[:, 0], op0=ALU.add, op1=ALU.mult)\
                        .then_inc(ln_step, 1)
                dve.wait_ge(ln_step, NS * g + 3 * NEWTON)
                nc.vector.tensor_tensor(ln_bias[:], ln_mean[:], ln_root[:, 3], ALU.mult).then_inc(ln_ready, 1)
                dve.wait_ge(ln_ready, g + 1)
                for b in range(1, GB):
                    nc.vector.tensor_scalar(y_nodes[parity][:, b], y_nodes[parity][:, b], ln_root[:, 3, b:b + 1],
                                            ln_bias[:, b:b + 1], ALU.mult, ALU.add).then_inc(normed_last, 1)

            dve.wait_ge(scalar_step, 6)
            dve.wait_ge(mask_made, 1)
            dve.wait_ge(mask_t_made, 1)
            iteration(0, 0, first=True)
            with dve.Fori(1, NG - 1, 2) as i:
                iteration(i, 1)
                iteration(i + 1, 0)
            last_iteration(LAST, 1)

        @block.gpsimd
        def _(pool):
            nc.gpsimd.memset(ident[:], 0.0).then_inc(ident_zeroed, 1)
            pool.wait_ge(ident_zeroed, 1)
            nc.gpsimd.affine_select(out=ident[:], in_=ident[:], compare_op=ALU.not_equal, fill=1.0, base=0,
                                    pattern=[[-1, P]], channel_multiplier=1).then_inc(ident_made, 1)

            def inverse_root(value_half, guess, out, step, base):
                for n in range(NEWTON):
                    at = base + 4 * n
                    if n:
                        pool.wait_ge(step, at)
                    nc.gpsimd.tensor_tensor(guess[:, 1], guess[:, 0], guess[:, 0], ALU.mult).then_inc(step, 1)
                    pool.wait_ge(step, at + 1)
                    nc.gpsimd.tensor_tensor(guess[:, 2], guess[:, 1], value_half, ALU.mult).then_inc(step, 1)
                    pool.wait_ge(step, at + 2)
                    nc.gpsimd.tensor_tensor(guess[:, 1], guess[:, 2], three_halves[:], ALU.add).then_inc(step, 1)
                    pool.wait_ge(step, at + 3)
                    nc.gpsimd.tensor_tensor(out if n == NEWTON - 1 else guess[:, 0], guess[:, 0], guess[:, 1],
                                            ALU.mult).then_inc(step, 1)
                pool.wait_ge(step, base + NS)

            def copy_x(g, parity, to_stored=True):
                for b in range(GB):
                    pool.wait_ge(xt_made, GB * g + b + 1)
                    if to_stored:
                        pool.wait_ge(y_stored[b], 16 * (g - 1))
                    nc.gpsimd.tensor_tensor(y_nodes[parity][:, b], x_nodes[parity][:, b],
                                            row_scale[:, 1, 0:1].broadcast_to([P, D]), ALU.mult).then_inc(x_copied, 1)

            def layernorm_factors(g, first=False):
                pool.wait_ge(ln_seed, g + 1)
                if not first:
                    pool.wait_ge(normed, GB * g)
                inverse_root(ln_var_half[:], ln_root, ln_root[:, 3], ln_step, NS * g)
                nc.gpsimd.tensor_tensor(ln_bias[:], ln_mean[:], ln_root[:, 3], ALU.mult).then_inc(ln_ready, 1)

            def node_scale(g):
                pool.wait_ge(root_seed, g + 1)
                inverse_root(square_half[:], root, row_scale[:, 0], root_step, NS * g)

            def edges_l(g):
                pool.wait_ge(mask_l_made, g + 1)
                pool.wait_ge(scale_loaded, 16 * (g + 1))
                nc.gpsimd.tensor_tensor(edges[:, 0], m_l[:], scale_rows[:], ALU.mult).then_inc(edges_l_made, 1)

            def scale_s(g):
                pool.wait_ge(s_made, g + 1)
                nc.gpsimd.tensor_tensor(s_scaled, s_l[:], row_scale[:, 0].unsqueeze(2).broadcast_to([P, GB, N]),
                                        ALU.mult).then_inc(s_scaled_made, 1)

            def scale_edges(g):
                pool.wait_ge(edges_t_made, 2 * (g + 1))
                pool.wait_ge(coef_loaded, 16 * (g + 1))
                nc.gpsimd.tensor_tensor(edges_t, edges_t, coef_rows, ALU.mult).then_inc(scaled_made, 1)

            def scale_last(g):
                pool.wait_ge(coef_made, g + 1)
                nc.gpsimd.tensor_tensor(edges[:, 1], edges[:, 1], coef[:, 2, 1].unsqueeze(2).broadcast_to([P, GB, N]),
                                        ALU.mult).then_inc(scaled_made, 1)

            pool.wait_ge(ones_made, 2)

            def iteration(g, parity, before=2, last=False):
                copy_x(g, parity, to_stored=before == 2)
                node_scale(g)
                scale_s(g)
                if last:
                    scale_last(g)
                    layernorm_factors(g - 1)
                else:
                    edges_l(g)
                    if before:
                        layernorm_factors(g - 1, first=before == 1)
                    scale_edges(g)

            pool.wait_ge(wot_made, C)
            iteration(0, 0, before=0)
            iteration(1, 1, before=1)
            with pool.Fori(2, LAST - 1, 2) as i:
                iteration(i, 0)
                iteration(i + 1, 1)
            iteration(LAST - 1, 0)
            iteration(LAST, 1, last=True)


_INS = ["x", "adj", "L0_gnn_W_lang", "L0_gnn_W_grav", "L0_gnn_W_V", "L0_gnn_W_O", "L0_gnn_gate_logit",
        "L0_gnn_log_sigma"]


def kernel(**inputs):
    import numpy as _np
    import concourse.bacc as _bacc
    from concourse.bass_utils import run_bass_kernel_spmd as _run

    nc = _bacc.Bacc("TRN2", target_bir_lowering=False, num_devices=1)
    arrays, args = {}, []
    for name in _INS:
        a = _np.ascontiguousarray(inputs[name])
        if a.ndim == 0:
            a = a.reshape(1)
        arrays[f"in_{name}"] = a
        args.append(nc.dram_tensor(f"in_{name}", a.shape, mybir.dt.from_np(a.dtype), kind="ExternalInput").ap())
    y = nc.dram_tensor("out_y", (B, N, D), F32, kind="ExternalOutput").ap()
    attention_layernorm(nc, *args, y)
    r = _run(nc, [arrays], core_ids=[0])
    return r.results[0]["out_y"]
```
